# Optimizing a Trainium2 kernel written in Bass

```python
import numpy as np
import jax
import jax.numpy as jnp

def _softmax(x, axis=-1):
    return jax.nn.softmax(x, axis=axis)

def _gelu(x):
    return jax.nn.gelu(x, approximate=True)

def _silu(x):
    return jax.nn.silu(x)

def _sigmoid(x):
    return jax.nn.sigmoid(x)

def _layernorm(x, axis=-1, eps=1e-05):
    m = jnp.mean(x, axis=axis, keepdims=True)
    v = jnp.var(x, axis=axis, keepdims=True)
    return (x - m) / jnp.sqrt(v + eps)

def _scatter_add(tgt, idx, src, axis=0):
    return tgt.at[idx].add(src)

def _segment_sum(src, seg, n):
    return jax.ops.segment_sum(src, seg, n)
kernel_name = 'mk_sandwich_d1_jaxref_r4_68d77b'

def setup_inputs(seed: int=0):
    np.random.seed(seed)
    _w = jnp.asarray

    def _L0_attn_setup():
        import jax, jax.numpy as jnp
        import numpy as np
        B, L, D_MODEL = (2, 256, 256)
        EXPAND = 2
        D_INNER = EXPAND * D_MODEL
        D_STATE = 16
        D_CONV = 4
        DT_RANK = D_MODEL // 16

        def _mamba(x, W_in, conv_w, conv_b, W_xproj, W_dt, b_dt, A_log, D_skip, W_out):
            b, l, _ = x.shape
            xz = jnp.einsum('bld,de->ble', x, W_in)
            x_in, z = jnp.split(xz, 2, axis=-1)
            xt = jnp.transpose(x_in, (0, 2, 1))
            xt = jnp.pad(xt, ((0, 0), (0, 0), (D_CONV - 1, 0)))
            conv = jax.lax.conv_general_dilated(xt, conv_w, window_strides=(1,), padding='VALID', dimension_numbers=('NCH', 'OIH', 'NCH'), feature_group_count=D_INNER)
            conv = conv + conv_b[None, :, None]
            u = jax.nn.silu(jnp.transpose(conv, (0, 2, 1)))
            x_dbl = jnp.einsum('bld,de->ble', u, W_xproj)
            dt_lr = x_dbl[..., :DT_RANK]
            Bm = x_dbl[..., DT_RANK:DT_RANK + D_STATE]
            Cm = x_dbl[..., DT_RANK + D_STATE:]
            delta = jax.nn.softplus(jnp.einsum('blr,rd->bld', dt_lr, W_dt) + b_dt)
            A = -jnp.exp(A_log)
            dA = jnp.exp(jnp.einsum('bld,dn->bldn', delta, A))
            dBu = (delta * u)[..., None] * Bm[:, :, None, :]

            def step(h, inp):
                dA_t, dBu_t, C_t = inp
                h = dA_t * h + dBu_t
                y_t = jnp.einsum('bdn,bn->bd', h, C_t)
                return (h, y_t)
            h0 = jnp.zeros((b, D_INNER, D_STATE), x.dtype)
            _, ys = jax.lax.scan(step, h0, (jnp.swapaxes(dA, 0, 1), jnp.swapaxes(dBu, 0, 1), jnp.swapaxes(Cm, 0, 1)))
            y = jnp.swapaxes(ys, 0, 1)
            y = y + D_skip * u
            y = y * jax.nn.silu(z)
            out = jnp.einsum('bld,de->ble', y, W_out)
            return out
        key = jax.random.key(seed)
        ks = jax.random.split(key, 8)
        s = 0.02
        x = jax.random.normal(ks[0], (B, L, D_MODEL), jnp.float32)
        W_in = jax.random.normal(ks[1], (D_MODEL, 2 * D_INNER), jnp.float32) * s
        conv_w = jax.random.normal(ks[2], (D_INNER, 1, D_CONV), jnp.float32) * 0.2
        conv_b = jnp.zeros((D_INNER,), jnp.float32)
        W_xproj = jax.random.normal(ks[3], (D_INNER, DT_RANK + 2 * D_STATE), jnp.float32) * s
        W_dt = jax.random.normal(ks[4], (DT_RANK, D_INNER), jnp.float32) * DT_RANK ** (-0.5)
        b_dt = jnp.full((D_INNER,), -4.6, jnp.float32)
        A_log = jnp.log(jnp.broadcast_to(jnp.arange(1, D_STATE + 1, dtype=jnp.float32), (D_INNER, D_STATE)))
        D_skip = jnp.ones((D_INNER,), jnp.float32)
        W_out = jax.random.normal(ks[5], (D_INNER, D_MODEL), jnp.float32) * s
        return dict(x=x, W_in=W_in, conv_w=conv_w, conv_b=conv_b, W_xproj=W_xproj, W_dt=W_dt, b_dt=b_dt, A_log=A_log, D_skip=D_skip, W_out=W_out)
    _L0_attn_in = _L0_attn_setup()

    def _L0_ffn_setup():
        import jax, jax.numpy as jnp
        import numpy as np
        TOP_K = 2
        NUM_EXPERTS = 8
        key = jax.random.key(seed)
        ks = jax.random.split(key, 8)
        h, d, ds, E = (256, 128, 256, NUM_EXPERTS)
        s = 1.0 / np.sqrt(h)
        return {'x': jax.random.normal(ks[0], (2, 512, h), jnp.float32), 'router': jax.random.normal(ks[1], (h, E), jnp.float32) * s, 'experts_gate': jax.random.normal(ks[2], (E, h, d), jnp.float32) * s, 'experts_up': jax.random.normal(ks[3], (E, h, d), jnp.float32) * s, 'experts_down': jax.random.normal(ks[4], (E, d, h), jnp.float32) * (1.0 / np.sqrt(d)), 'shared_gate': jax.random.normal(ks[5], (h, ds), jnp.float32) * s, 'shared_up': jax.random.normal(ks[6], (h, ds), jnp.float32) * s, 'shared_down': jax.random.normal(ks[7], (ds, h), jnp.float32) * (1.0 / np.sqrt(ds))}
    _L0_ffn_in = _L0_ffn_setup()
    _d = {'L0_attn_x': _L0_attn_in['x'], 'L0_attn_W_in': _L0_attn_in['W_in'], 'L0_attn_conv_w': _L0_attn_in['conv_w'], 'L0_attn_conv_b': _L0_attn_in['conv_b'], 'L0_attn_W_xproj': _L0_attn_in['W_xproj'], 'L0_attn_W_dt': _L0_attn_in['W_dt'], 'L0_attn_b_dt': _L0_attn_in['b_dt'], 'L0_attn_A_log': _L0_attn_in['A_log'], 'L0_attn_D_skip': _L0_attn_in['D_skip'], 'L0_attn_W_out': _L0_attn_in['W_out'], 'L0_ffn_router': _L0_ffn_in['router'], 'L0_ffn_experts_gate': _L0_ffn_in['experts_gate'], 'L0_ffn_experts_up': _L0_ffn_in['experts_up'], 'L0_ffn_experts_down': _L0_ffn_in['experts_down'], 'L0_ffn_shared_gate': _L0_ffn_in['shared_gate'], 'L0_ffn_shared_up': _L0_ffn_in['shared_up'], 'L0_ffn_shared_down': _L0_ffn_in['shared_down']}
    _x0 = _d['L0_attn_x']
    _d['L0_attn_x'] = jax.random.normal(jax.random.fold_in(jax.random.key(seed), 1), (2, 4096, 256), dtype=_x0.dtype)
    del _x0
    return _d

def reference(L0_attn_x, L0_attn_W_in, L0_attn_conv_w, L0_attn_conv_b, L0_attn_W_xproj, L0_attn_W_dt, L0_attn_b_dt, L0_attn_A_log, L0_attn_D_skip, L0_attn_W_out, L0_ffn_router, L0_ffn_experts_gate, L0_ffn_experts_up, L0_ffn_experts_down, L0_ffn_shared_gate, L0_ffn_shared_up, L0_ffn_shared_down):

    def _L0_attn_ref(x, W_in, conv_w, conv_b, W_xproj, W_dt, b_dt, A_log, D_skip, W_out):
        import jax, jax.numpy as jnp
        import numpy as np
        B, L, D_MODEL = (2, 256, 256)
        EXPAND = 2
        D_INNER = EXPAND * D_MODEL
        D_STATE = 16
        D_CONV = 4
        DT_RANK = D_MODEL // 16

        def _mamba(x, W_in, conv_w, conv_b, W_xproj, W_dt, b_dt, A_log, D_skip, W_out):
            b, l, _ = x.shape
            xz = jnp.einsum('bld,de->ble', x, W_in)
            x_in, z = jnp.split(xz, 2, axis=-1)
            xt = jnp.transpose(x_in, (0, 2, 1))
            xt = jnp.pad(xt, ((0, 0), (0, 0), (D_CONV - 1, 0)))
            conv = jax.lax.conv_general_dilated(xt, conv_w, window_strides=(1,), padding='VALID', dimension_numbers=('NCH', 'OIH', 'NCH'), feature_group_count=D_INNER)
            conv = conv + conv_b[None, :, None]
            u = jax.nn.silu(jnp.transpose(conv, (0, 2, 1)))
            x_dbl = jnp.einsum('bld,de->ble', u, W_xproj)
            dt_lr = x_dbl[..., :DT_RANK]
            Bm = x_dbl[..., DT_RANK:DT_RANK + D_STATE]
            Cm = x_dbl[..., DT_RANK + D_STATE:]
            delta = jax.nn.softplus(jnp.einsum('blr,rd->bld', dt_lr, W_dt) + b_dt)
            A = -jnp.exp(A_log)
            dA = jnp.exp(jnp.einsum('bld,dn->bldn', delta, A))
            dBu = (delta * u)[..., None] * Bm[:, :, None, :]

            def step(h, inp):
                dA_t, dBu_t, C_t = inp
                h = dA_t * h + dBu_t
                y_t = jnp.einsum('bdn,bn->bd', h, C_t)
                return (h, y_t)
            h0 = jnp.zeros((b, D_INNER, D_STATE), x.dtype)
            _, ys = jax.lax.scan(step, h0, (jnp.swapaxes(dA, 0, 1), jnp.swapaxes(dBu, 0, 1), jnp.swapaxes(Cm, 0, 1)))
            y = jnp.swapaxes(ys, 0, 1)
            y = y + D_skip * u
            y = y * jax.nn.silu(z)
            out = jnp.einsum('bld,de->ble', y, W_out)
            return out
        return _mamba(x, W_in, conv_w, conv_b, W_xproj, W_dt, b_dt, A_log, D_skip, W_out)

    def _L0_ffn_ref(x, router, experts_gate, experts_up, experts_down, shared_gate, shared_up, shared_down):
        import jax, jax.numpy as jnp
        import numpy as np
        TOP_K = 2
        NUM_EXPERTS = 8
        b, s, h = x.shape
        E = router.shape[1]
        shared_act = jax.nn.silu(jnp.einsum('bsh,hd->bsd', x, shared_gate))
        shared_up_out = jnp.einsum('bsh,hd->bsd', x, shared_up)
        shared_out = jnp.einsum('bsd,dh->bsh', shared_act * shared_up_out, shared_down)
        router_probs = jax.nn.softmax(jnp.einsum('bsh,he->bse', x, router), axis=-1)
        topk_probs, topk_idx = jax.lax.top_k(router_probs, TOP_K)
        coef = jnp.sum(jax.nn.one_hot(topk_idx, E, dtype=x.dtype) * topk_probs[..., None], axis=2)
        coef = coef.reshape(b * s, E)
        x_flat = x.reshape(b * s, h)
        gate = jnp.einsum('th,ehd->etd', x_flat, experts_gate)
        up = jnp.einsum('th,ehd->etd', x_flat, experts_up)
        expert_out = jnp.einsum('etd,edh->eth', jax.nn.silu(gate) * up, experts_down)
        routed = jnp.einsum('eth,te->th', expert_out, coef)
        return routed.reshape(b, s, h) + shared_out
    x = L0_attn_x
    x = x + _layernorm(_L0_attn_ref(_layernorm(x, axis=-1), L0_attn_W_in, L0_attn_conv_w, L0_attn_conv_b, L0_attn_W_xproj, L0_attn_W_dt, L0_attn_b_dt, L0_attn_A_log, L0_attn_D_skip, L0_attn_W_out), axis=-1)
    x = x + _layernorm(_L0_ffn_ref(_layernorm(x, axis=-1), L0_ffn_router, L0_ffn_experts_gate, L0_ffn_experts_up, L0_ffn_experts_down, L0_ffn_shared_gate, L0_ffn_shared_up, L0_ffn_shared_down), axis=-1)
    return x

_drawn_inputs = setup_inputs


def setup_inputs(seed=0):
    import zlib

    import numpy as np

    out = dict(_drawn_inputs(seed))
    spreads = {'L0_attn_conv_b': (0.0, 0.1),
     'L0_attn_b_dt': (-4.599999904632568, 0.6),
     'L0_attn_D_skip': (1.0, 0.2)}
    factors = {'L0_attn_W_xproj': 8.0, 'L0_attn_W_dt': 8.0, 'L0_attn_A_log': 8.0}
    for name, (base, spread) in spreads.items():
        noise = np.random.default_rng([zlib.crc32(name.encode()), seed]).standard_normal(out[name].shape)
        drawn = base * np.exp(spread * noise) if base else spread * noise
        out[name] = jnp.asarray(drawn.astype(out[name].dtype))
    for name, factor in factors.items():
        out[name] = (out[name] * factor).astype(out[name].dtype)
    return out
```

```python
from contextlib import ExitStack

import concourse.bass as bass
from concourse import mybir


class Stage:

    def __init__(self, sem, per):
        self.sem, self.per = sem, per

    def at(self, chunk, k=None):
        value = chunk * self.per + (self.per if k is None else k)
        return max(value, 0) if isinstance(value, int) else value


def mamba_moe_kernel(nc, x, w_in, conv_w, conv_b, w_xproj, w_dt, b_dt, a_log, d_skip, w_out,
                     router, e_gate, e_up, e_down, s_gate, s_up, s_down, out):
    f32, f32r = mybir.dt.float32, mybir.dt.float32r
    ALU, ACT, X = mybir.AluOpType, mybir.ActivationFunctionType, mybir.AxisListType.X
    P = 128
    BATCH, LENGTH, DM = x.shape
    DI, TAPS = conv_w.shape[0], conv_w.shape[2]
    NS = a_log.shape[1]
    RANK = w_dt.shape[0]
    E = router.shape[1]
    T = 512
    NT = T // P
    KM = DM // P
    J = DI // P
    SH = s_gate.shape[1] // P
    F = SH + E
    CHUNKS = BATCH * LENGTH // T
    EPS = 1e-5
    ROW_B, ROW_B2, ROW_DT, ROW_C = 0, 32, 64, 96
    XD_ROWS = ROW_C + NS
    ROW_K, ROW_K2 = 64, 96
    KC = ROW_B2 + E

    with ExitStack() as ctx:
        def sb(name, shape, dt=f32):
            return ctx.enter_context(nc.sbuf_tensor(name, shape, dt))

        def ps(name):
            return ctx.enter_context(nc.psum_tensor(name, [P, 512], f32))

        def stage(name, per):
            return Stage(ctx.enter_context(nc.semaphore(name)), per)

        WIN = sb("w_in_sb", [P, KM, 2 * DI])
        WG = sb("w_gate_sb", [P, KM, F, P])
        WU = sb("w_up_sb", [P, KM, F, P])
        WD = sb("w_down_sb", [P, F, DM])
        WO = sb("w_out_sb", [P, J, DM])
        WX = sb("w_xproj_sb", [P, J, XD_ROWS])
        WDT = sb("w_dt_sb", [P, DI])
        WR = sb("router_sb", [P, KM, E])
        CW = sb("conv_w_sb", [P, J, TAPS])
        CB_ = sb("conv_b_sb", [P, J])
        BDT = sb("b_dt_sb", [P, J])
        DSK = sb("d_skip_sb", [P, J])
        ANEG = sb("a_neg", [P, J, NS])
        EPST = sb("eps", [P, 1])
        IDN = sb("ident", [P, P])
        DIAG = sb("diag_d", [P, J, P])
        SEL = sb("sel", [P, NS], f32r)
        RANKS = sb("ranks", [P, E])
        XA = sb("xa", [P, NT, DM])
        ZB = sb("z_buf", [P, J, T])
        XN = ZB[:, 0:2, :].rearrange("p j t -> p (j t)").rearrange("p (a d) -> p a d", a=NT)
        XT = ZB[:, 2:4, :]
        SCR = sb("scratch", [P, J, T])
        XIN = sb("xin", [P, J, T + TAPS - 1])
        HALO = sb("halo", [P, BATCH, J, TAPS - 1])
        U = sb("u", [P, J, T])
        TC = sb("tanh_conv", [P, T])
        TZ = sb("tanh_z", [P, T])
        ZC = sb("z_copy", [P, T])
        SZ = sb("silu_z", [P, 2, NT, DI])
        DL = sb("delta", [P, 2, J, T])
        DU = sb("delta_u", [P, J, T])
        XD = sb("x_dbl", [P, T])
        HL = sb("hi_lo", [P, 2, T], f32r)
        CT = sb("c_t", [P, 2, NT, NS])
        BB = sb("b_rows", [P, 2, T])
        DA = sb("d_a", [P, J, T])
        BU = sb("d_bu", [P, 4, 2, T])
        H = sb("h", [P, 2, J, T])
        CARRY = sb("carry", [P, BATCH, NS, J])
        YT = sb("y_t", [P, NT, DI])
        XR = sb("xr", [P, NT, DM])
        X1T = sb("x1_t", [P, KM, T])
        TG = sb("tanh_gate", [P, T])
        HF = sb("hidden", [P, T])
        UP = sb("up", [P, T])
        CB = sb("coef_rows", [P, T])
        ST = {w: sb(f"stats_{w}", [P, NT, 6]) for w in ("xa", "o")}
        ST["x1"] = ST["y"] = ST["o"]
        MV = {w: sb(f"mean_var_{w}", [P, NT, 2]) for w in ("xa", "o", "x1", "y")}
        RS = {w: sb(f"rstd_{w}", [P, NT]) for w in ("xa", "o", "x1", "y")}
        R_SMALL = sb("r_small", [P, 4, NT])
        RMAX, RSUM, RINV, R1 = (R_SMALL[:, i, :] for i in range(4))
        RP = sb("r_prob", [P, NT, E])
        RQ = sb("r_equal", [P, NT, E])
        RM = sb("r_mask", [P, NT, E])
        RL = sb("r_left", [P, NT, E])
        SELF = RQ[:, :, :].rearrange("p a e -> p (a e)")[:, 0:NS]
        COEF = sb("coef", [P, NT, KC])

        HT = [ps("ht0"), ps("ht1")]
        DN = [ps("dn0"), ps("dn1")]
        BK = ps("b_bank")
        GK = ps("gate_bank")
        RING = [ps("ring0"), ps("ring1")]

        const_ld, xa_ld = stage("const_ld", 0), stage("xa_ld", 16)
        xr_ld, out_st = stage("xr_ld", 16), stage("out_st", 16)
        zeroed, ident_made, consts = stage("zeroed", 0), stage("ident_made", 0), stage("consts", 0)
        a_exp = stage("a_exp", 0)
        bk_full, ht_full = stage("bk_full", NS), stage("ht_full", NT * (NS + 1))
        full = {w: stage(f"{w}_full", n) for w, n in dict(
            yd=J, xt=KM, xin=J, z=NT, x1t=KM, up=F, cf=1, cb=E, xd=1, ct=1, dl=J).items()}
        o_full, rt_full = stage("o_full", NT), stage("rt_full", 1)
        gate_full, down = stage("gate_full", F), stage("down", F)
        bb, ex = stage("bb", NS), stage("ex", NS * J)
        yd, yinit, xt = stage("yd", J), stage("yinit", NT), stage("xt", KM)
        rstd = {w: stage(f"rstd_{w}_s", 2) for w in ("xa", "o", "x1", "y")}
        halo, xin, tz = stage("halo_s", 2), stage("xin_s", J), stage("tz_s", 2 * NT)
        x1t, tc, tg, up = stage("x1t_s", KM), stage("tc_s", J), stage("tg_s", F), stage("up_s", F)
        rex, cff, cfh, cb = stage("rex", 1), stage("cff", 1), stage("cfh", 1), stage("cb_s", E)
        xd, bhi, ct = stage("xd_s", 1), stage("bhi", 1), stage("ct_s", 1)
        absrelu, zex, ln = stage("absrelu", 2 * J), stage("zex", 1), stage("ln", 1)
        scan, add_c, carry = stage("scan", NS * J), stage("add_c", NS * NT), stage("carry_s", NS)
        stats = {w: stage(f"stats_{w}_s", 2 * NT) for w in ("xa", "o", "x1", "y")}
        norm = {w: stage(f"norm_{w}", NT) for w in ("xa", "o", "x1", "y")}
        y_add, y_gate = stage("y_add", 1), stage("y_gate", NT)
        conv, u_s, sz = stage("conv", J * TAPS), stage("u_s", J), stage("sz", NT)
        RT_STEPS = 19
        rt = stage("rt", RT_STEPS)
        hid, cflo, blo = stage("hid", F), stage("cflo", 1), stage("blo", 1)
        lsum, w1 = stage("lsum", J), stage("w1", J)
        waited = ctx.enter_context(nc.semaphore("waited"))
        bu, x1_add = stage("bu", 2 * NS), stage("x1_add", 1)
        hf = stage("hf", SH + 2 * E)
        zc, dadd, du = stage("zc", J), stage("dadd", J), stage("du", J)

        def hf_done(k):
            return k + 1 if k < SH else SH + 2 * (k + 1 - SH)

        FS = 5
        RING_USE = [("yd", -1, j) for j in range(J)]
        RING_USE += [("xt", 1, k) for k in range(KM)]
        RING_USE += [("xin", 1, 0), ("xin", 1, 1), ("z", 1, 0)]
        RING_USE += [("x1t", -1, k) for k in range(KM)] + [("xin", 1, 2), ("xin", 1, 3)]
        RING_USE += [("up", -1, 0), ("up", -1, 1), ("z", 1, 1)]
        RING_USE += [("cf", -1, 0), ("up", -1, 2), ("z", 1, 2), ("cb", -1, 0)]
        RING_USE += [("up", -1, 3), ("cb", -1, 1), ("z", 1, 3), ("xd", 1, 0)]
        RING_USE += [("up", -1, 4), ("cb", -1, 2), ("ct", 1, 0), ("dl", 1, 0), ("dl", 1, 1)]
        RING_USE += [("up", -1, 5), ("cb", -1, 3), ("dl", 1, 2), ("dl", 1, 3)]
        for k in range(6, F):
            RING_USE += [("up", -1, k), ("cb", -1, k - SH)]
        ring_free = {"yd": (yd, 1), "xt": (xt, 1), "xin": (xin, 1), "z": (tz, 2), "x1t": (x1t, 1),
                     "up": (up, 1), "cf": (cff, 1), "cb": (cb, 1), "xd": (xd, 1), "ct": (ct, 1),
                     "dl": (absrelu, 2)}

        def ring_bank(what, k):
            at = next(i for i, use in enumerate(RING_USE) if use[0] == what and use[2] == k)
            return RING[at % 2]

        def ring_user_before(s, lo, what, k):
            at = next(i for i, use in enumerate(RING_USE) if use[0] == what and use[2] == k)
            back, parity = 0, at % 2
            while lo - back >= -1:
                at -= 1
                if at < 0:
                    at, back = len(RING_USE) - 1, back + 1
                before, part, kb = RING_USE[at]
                if at % 2 == parity and 0 <= lo - back + part < CHUNKS:
                    freed, per = ring_free[before]
                    return freed.sem, freed.at(s - back + part, per * (kb + 1))
            return yd.sem, 0

        bodies_before = [-1, 0, 1]
        loop_first, loop_last = 2, CHUNKS - 3
        bodies_after = [CHUNKS - 2, CHUNKS - 1, CHUNKS]

        def run(engine, body):
            for s in bodies_before:
                body(s, s, s % 2)
            with engine.Fori(0, (loop_last - loop_first + 1) // 2) as i:
                for r in range(2):
                    body(2 * i + loop_first + r, loop_first + r, r)
            for s in bodies_after:
                body(s, s, s % 2)

        def parts(lo):
            return 0 <= lo < CHUNKS, 0 <= lo - 1 < CHUNKS, 0 <= lo + 1 < CHUNKS

        def tokens(dram, batch, index):
            return dram[batch, bass.ds(index * T, T), :].rearrange("(a p) d -> p a d", p=P)

        block = ctx.enter_context(nc.Block())

        @block.sync
        def _(sp):
            loads = [
                (WIN[:, :, :], w_in.rearrange("(k p) c -> p k c", p=P)),
                (CW[:, :, :], conv_w.rearrange("(j p) o k -> p j (o k)", p=P)),
                (CB_[:, :], conv_b.rearrange("(j p) -> p j", p=P)),
                (BDT[:, :], b_dt.rearrange("(j p) -> p j", p=P)),
                (DSK[:, :], d_skip.rearrange("(j p) -> p j", p=P)),
                (ANEG[:, :, :], a_log.rearrange("(j p) n -> p j n", p=P)),
                (WDT[ROW_DT:ROW_DT + RANK, :], w_dt),
                (WO[:, :, :], w_out.rearrange("(j p) c -> p j c", p=P)),
                (WR[:, :, :], router.rearrange("(k p) e -> p k e", p=P)),
            ]
            for k in range(KM):
                rows = slice(k * P, (k + 1) * P)
                for dst, shared, experts in ((WG, s_gate, e_gate), (WU, s_up, e_up)):
                    loads.append((dst[:, k, 0:SH, :], shared[rows, :].rearrange("p (g f) -> p g f", g=SH)))
                    loads.append((dst[:, k, SH:F, :], experts[:, rows, :].rearrange("e p f -> p e f")))
            loads.append((WD[:, 0:SH, :], s_down.rearrange("(g p) c -> p g c", p=P)))
            loads.append((WD[:, SH:F, :], e_down.rearrange("e p c -> p e c")))
            sp.dma_start(XA[:, :, :], tokens(x, 0, 0)).then_inc(xa_ld.sem, 16)
            with nc.allow_non_contiguous_dma(reason="512 values each"):
                for dst, src in loads:
                    sp.dma_start(dst, src).then_inc(const_ld.sem, 16)
            sp.wait_ge(zeroed.sem, 1)
            wx = w_xproj.rearrange("(j p) c -> p j c", p=P)
            for row, col in ((ROW_B, RANK), (ROW_B2, RANK), (ROW_DT, 0), (ROW_C, RANK + NS)):
                width = RANK if row == ROW_DT else NS
                sp.dma_start(WX[:, :, row:row + width], wx[:, :, col:col + width])\
                  .then_inc(const_ld.sem, 16)

            def body(s, lo, r):
                _, ffn, _ = parts(lo)
                if ffn:
                    sp.wait_ge(out_st.sem, out_st.at(s - 2))
                    sp.dma_start(XR[:, :, :], tokens(x, 1 - r, (s - 1 - (1 - r)) // 2))\
                      .then_inc(xr_ld.sem, 16)
                if 0 <= lo + 2 < CHUNKS:
                    sp.wait_ge(full["xt"].sem, full["xt"].at(s + 1))
                    sp.dma_start(XA[:, :, :], tokens(x, r, (s + 2 - r) // 2)).then_inc(xa_ld.sem, 16)
                if ffn:
                    sp.wait_ge(y_add.sem, y_add.at(s - 1))
                    sp.dma_start(tokens(out, 1 - r, (s - 1 - (1 - r)) // 2), XR[:, :, :])\
                      .then_inc(out_st.sem, 16)

            for s in bodies_before:
                body(s, s, s % 2)
            with sp.Fori(0, (loop_last - loop_first + 1) // 2) as i:
                for r in range(2):
                    s = 2 * i + loop_first + r
                    sp.wait_ge(out_st.sem, out_st.at(s - 2))
                    sp.dma_start(XR[:, :, :], tokens(x, 1 - r, i + (loop_first + 2 * r - 2) // 2))\
                      .then_inc(xr_ld.sem, 16)
                    sp.wait_ge(full["xt"].sem, full["xt"].at(s + 1))
                    sp.dma_start(XA[:, :, :], tokens(x, r, i + (loop_first + 2) // 2)).then_inc(xa_ld.sem, 16)
                    sp.wait_ge(y_add.sem, y_add.at(s - 1))
                    sp.dma_start(tokens(out, 1 - r, i + (loop_first + 2 * r - 2) // 2), XR[:, :, :])\
                      .then_inc(out_st.sem, 16)
            for s in bodies_after:
                body(s, s, s % 2)
            sp.wait_ge(out_st.sem, out_st.at(CHUNKS - 1))

        IDENT_MADE = 3 + P // 32 + E
        CONST_LOADS = (9 + 4 * KM + 2 + 4) * 16

        @block.tensor
        def _(pe):
            pe.wait_ge(consts.sem, 1)
            pe.wait_ge(const_ld.sem, CONST_LOADS)
            pe.wait_ge(ident_made.sem, IDENT_MADE)

            def b_rows(s, r, n):
                pe.wait_ge(bb.sem, bb.at(s, n))
                nc.tensor.matmul(BK[:, :], SEL[0:ROW_B2 + NS, n:n + 1].to_broadcast([ROW_B2 + NS, P]),
                                 HL[0:ROW_B2 + NS, r, :], start=True, stop=True)\
                  .then_inc(bk_full.sem, 1)

            def ht_user_before(s, q):
                if q < 2:
                    return add_c.sem, add_c.at(s - 1, NS * NT - 1 + q)
                if q < NT + 2:
                    return yinit.sem, yinit.at(s, q - 1)
                return add_c.sem, add_c.at(s, q - NT - 1)

            def body(s, lo, r):
                with_scan, ffn, prep = parts(lo)
                o = 1 - r
                if with_scan:
                    pe.wait_ge(blo.sem, blo.at(s))
                    b_rows(s, r, 0)
                    b_rows(s, r, 1)
                for n in range(NS):
                    if with_scan and n + 2 < NS:
                        b_rows(s, r, n + 2)
                    if with_scan and n > 0:
                        transpose_state(s, n - 1)
                    if ffn:
                        ffn_part(s, lo, o, n)
                    if n == 0 and with_scan:
                        for a in range(NT):
                            pe.wait_ge(*ht_user_before(s, a))
                            for j in range(J):
                                last = nc.tensor.matmul(HT[a % 2][:, j * P:(j + 1) * P],
                                                        U[:, j, a * P:(a + 1) * P], DIAG[:, j, :],
                                                        start=True, stop=True)
                            last.then_inc(ht_full.sem, 1)
                    if prep:
                        prep_part(s, lo, o, n)
                    if ffn and n == FS + SH:
                        coef_rows(s, lo, o, 0)
                if with_scan:
                    transpose_state(s, NS - 1)

            def transpose_state(s, n):
                pe.wait_ge(scan.sem, scan.at(s, (n + 1) * J))
                for a in range(NT):
                    q = NT * (n + 1) + a
                    pe.wait_ge(*ht_user_before(s, q))
                    for j in range(J):
                        last = nc.tensor.transpose(HT[q % 2][:, j * P:(j + 1) * P],
                                                   H[:, n % 2, j, a * P:(a + 1) * P], IDN[:, :])
                    last.then_inc(ht_full.sem, 1)

            def ffn_part(s, lo, o, n):
                c = s - 1
                if n == 0:
                    pe.wait_ge(y_gate.sem, y_gate.at(c))
                    for j in range(J):
                        pe.wait_ge(*ring_user_before(s, lo, "yd", j))
                        bank = ring_bank("yd", j)
                        for a in range(NT):
                            last = nc.tensor.transpose(bank[:, a * P:(a + 1) * P],
                                                       YT[:, a, j * P:(j + 1) * P], IDN[:, :])
                        last.then_inc(full["yd"].sem, 1)
                if n == 1:
                    pe.wait_ge(yd.sem, yd.at(c))
                    pe.wait_ge(norm["y"].sem, norm["y"].at(c - 1))
                    for a in range(NT):
                        for j in range(J):
                            last = nc.tensor.matmul(DN[a // 2][:, (a % 2) * DM:(a % 2 + 1) * DM],
                                                    SCR[:, j, a * P:(a + 1) * P], WO[:, j, :],
                                                    start=(j == 0), stop=(j == J - 1))
                        last.then_inc(o_full.sem, 1)
                if n == 4:
                    pe.wait_ge(norm["x1"].sem, norm["x1"].at(c))
                    for k in range(KM):
                        pe.wait_ge(*ring_user_before(s, lo, "x1t", k))
                        bank = ring_bank("x1t", k)
                        for a in range(NT):
                            last = nc.tensor.transpose(bank[:, a * P:(a + 1) * P],
                                                       XN[:, a, k * P:(k + 1) * P], IDN[:, :])
                        last.then_inc(full["x1t"].sem, 1)
                if n == FS:
                    pe.wait_ge(x1t.sem, x1t.at(c))
                    pe.wait_ge(norm["o"].sem, norm["o"].at(c))
                    for a in range(NT):
                        for k in range(KM):
                            last = nc.tensor.matmul(DN[0][:, a * E:(a + 1) * E],
                                                    X1T[:, k, a * P:(a + 1) * P], WR[:, k, :],
                                                    start=(k == 0), stop=(k == KM - 1))
                    last.then_inc(rt_full.sem, 1)
                if n == FS + SH:
                    pe.wait_ge(rt.sem, rt.at(c))
                    pe.wait_ge(*ring_user_before(s, lo, "cf", 0))
                    bank = ring_bank("cf", 0)
                    for a in range(NT):
                        last = nc.tensor.matmul(bank[0:KC, a * P:(a + 1) * P], COEF[:, a, :],
                                                IDN[:, :], start=True, stop=True)
                    last.then_inc(full["cf"].sem, 1)
                f = n - FS
                if 0 <= f - 1 < F:
                    down_part(c, f - 1)
                if 0 <= f < F:
                    pe.wait_ge(hid.sem, hid.at(c, f))
                    for k in range(KM):
                        last = nc.tensor.matmul(GK[:, :], WG[:, k, f, :], X1T[:, k, :],
                                                start=(k == 0), stop=(k == KM - 1))
                    last.then_inc(gate_full.sem, 1)
                    pe.wait_ge(*ring_user_before(s, lo, "up", f))
                    bank = ring_bank("up", f)
                    for k in range(KM):
                        last = nc.tensor.matmul(bank[:, :], WU[:, k, f, :], X1T[:, k, :],
                                                start=(k == 0), stop=(k == KM - 1))
                    last.then_inc(full["up"].sem, 1)
                    if f > SH:
                        coef_rows(s, lo, o, f - SH)

            def coef_rows(s, lo, o, e):
                pe.wait_ge(cflo.sem, cflo.at(s - 1))
                pe.wait_ge(*ring_user_before(s, lo, "cb", e))
                nc.tensor.matmul(ring_bank("cb", e)[:, :],
                                 SEL[ROW_K:ROW_K + KC, e:e + 1].to_broadcast([KC, P]),
                                 HL[ROW_K:ROW_K + KC, o, :], start=True, stop=True)\
                  .then_inc(full["cb"].sem, 1)

            def down_part(c, f):
                pe.wait_ge(hf.sem, hf.at(c, hf_done(f)))
                if f == 0:
                    pe.wait_ge(rt.sem, rt.at(c, 2))
                for a in range(NT):
                    last = nc.tensor.matmul(DN[a // 2][:, (a % 2) * DM:(a % 2 + 1) * DM],
                                            HF[:, a * P:(a + 1) * P], WD[:, f, :],
                                            start=(f == 0 and a % 2 == 0), stop=(f == F - 1),
                                            skip_group_check=True)
                last.then_inc(down.sem, 1)

            def prep_part(s, lo, o, n):
                c = s + 1

                def x_in(j):
                    pe.wait_ge(*ring_user_before(s, lo, "xin", j))
                    for k in range(KM):
                        last = nc.tensor.matmul(ring_bank("xin", j)[:, :], WIN[:, k, j * P:(j + 1) * P],
                                                XT[:, k, :], start=(k == 0), stop=(k == KM - 1))
                    last.then_inc(full["xin"].sem, 1)

                def z(a):
                    pe.wait_ge(*ring_user_before(s, lo, "z", a))
                    for k in range(KM):
                        last = nc.tensor.matmul(ring_bank("z", a)[:, :], XT[:, k, a * P:(a + 1) * P],
                                                WIN[:, k, DI:2 * DI], start=(k == 0), stop=(k == KM - 1))
                    last.then_inc(full["z"].sem, 1)

                def delta(j):
                    pe.wait_ge(*ring_user_before(s, lo, "dl", j))
                    nc.tensor.matmul(ring_bank("dl", j)[:, :], WDT[ROW_DT:ROW_DT + RANK, j * P:(j + 1) * P],
                                     XD[ROW_DT:ROW_DT + RANK, :], start=True, stop=True)\
                      .then_inc(full["dl"].sem, 1)

                if n == 2:
                    pe.wait_ge(norm["xa"].sem, norm["xa"].at(c))
                    for k in range(KM):
                        pe.wait_ge(*ring_user_before(s, lo, "xt", k))
                        for a in range(NT):
                            last = nc.tensor.transpose(ring_bank("xt", k)[:, a * P:(a + 1) * P],
                                                       XA[:, a, k * P:(k + 1) * P], IDN[:, :])
                        last.then_inc(full["xt"].sem, 1)
                if n == 3:
                    pe.wait_ge(xt.sem, xt.at(c))
                    x_in(0)
                    x_in(1)
                    z(0)
                if n == 4:
                    x_in(2)
                    x_in(3)
                if n in (6, 7, 8):
                    z(n - 5)
                if n == 8:
                    pe.wait_ge(u_s.sem, u_s.at(c))
                    pe.wait_ge(*ring_user_before(s, lo, "xd", 0))
                    for j in range(J):
                        last = nc.tensor.matmul(ring_bank("xd", 0)[0:XD_ROWS, :], WX[:, j, :], U[:, j, :],
                                                start=(j == 0), stop=(j == J - 1))
                    last.then_inc(full["xd"].sem, 1)
                if n == 9:
                    pe.wait_ge(xd.sem, xd.at(c))
                    pe.wait_ge(*ring_user_before(s, lo, "ct", 0))
                    for a in range(NT):
                        last = nc.tensor.matmul(ring_bank("ct", 0)[:, a * NS:(a + 1) * NS],
                                                XD[ROW_C:ROW_C + NS, a * P:(a + 1) * P],
                                                IDN[ROW_C:ROW_C + NS, ROW_C:ROW_C + NS],
                                                start=True, stop=True)
                    last.then_inc(full["ct"].sem, 1)
                    delta(0)
                    delta(1)
                if n == 10:
                    delta(2)
                    delta(3)

            run(pe, body)

        @block.scalar
        def _(act):
            act.wait_ge(const_ld.sem, CONST_LOADS)
            nc.scalar.activation(ANEG[:, :, :], ANEG[:, :, :], ACT.Exp).then_inc(a_exp.sem, 1)
            act.wait_ge(consts.sem, 1)

            def b_take(s, n):
                act.wait_ge(bk_full.sem, bk_full.at(s, n + 1))
                if n < 2:
                    act.wait_ge(bu.sem, bu.at(s - 1, 2 * (n + NS - 2) + 2))
                else:
                    act.wait_ge(bu.sem, bu.at(s, 2 * (n - 2) + 2))
                nc.scalar.activation(BB[:, n % 2, :], BK[:, :], ACT.Copy).then_inc(bb.sem, 1)

            def decay(s, r, n):
                for j in range(J):
                    if n == 0:
                        act.wait_ge(scan.sem, scan.at(s - 1, (NS - 1) * J + j + 1))
                        act.wait_ge(dadd.sem, dadd.at(s, j + 1))
                    else:
                        act.wait_ge(scan.sem, scan.at(s, (n - 1) * J + j + 1))
                    nc.scalar.activation(DA[:, j, :], DL[:, r, j, :], ACT.Exp,
                                         scale=ANEG[:, j, n:n + 1]).then_inc(ex.sem, 1)

            def rsqrt(w, c):
                act.wait_ge(stats[w].sem, stats[w].at(c))
                act.wait_ge(norm[w].sem, norm[w].at(c - 1))
                nc.scalar.activation(RS[w][:, :], MV[w][:, :, 1], ACT.Ln, bias=EPST[:, 0:1])\
                  .then_inc(rstd[w].sem, 1)
                act.wait_ge(rstd[w].sem, rstd[w].at(c, 1))
                nc.scalar.activation(RS[w][:, :], RS[w][:, :], ACT.Exp, scale=-0.5)\
                  .then_inc(rstd[w].sem, 1)

            def body(s, lo, r):
                with_scan, ffn, prep = parts(lo)
                o = 1 - r
                if with_scan:
                    b_take(s, 0)
                    b_take(s, 1)
                    decay(s, r, 0)
                for n in range(NS):
                    if ffn and n == FS + 1:
                        act.wait_ge(rt.sem, rt.at(s - 1, 2))
                        nc.scalar.activation(RP[:, :, :], RP[:, :, :], ACT.Exp).then_inc(rex.sem, 1)
                    if with_scan and n + 2 < NS:
                        b_take(s, n + 2)
                    if with_scan and n + 1 < NS:
                        decay(s, r, n + 1)
                    if ffn:
                        ffn_part(s, lo, o, n)
                    if with_scan and n == 0:
                        for a in range(NT):
                            act.wait_ge(ht_full.sem, ht_full.at(s, a + 1))
                            act.wait_ge(full["yd"].sem, full["yd"].at(s - 1))
                            nc.scalar.activation(YT[:, a, :], HT[a % 2][:, :], ACT.Copy)\
                              .then_inc(yinit.sem, 1)
                    if prep:
                        prep_part(s, lo, o, n)
                    if ffn and n == 3:
                        rsqrt("x1", s - 1)
                    if ffn and n == FS + SH:
                        coef_take(s - 1, 0)
                if ffn:
                    rsqrt("y", s - 1)

            def coef_take(c, e):
                act.wait_ge(full["cb"].sem, full["cb"].at(c, e + 1))
                k = SH + e
                act.wait_ge(hf.sem, hf.at(c, hf_done(k - 1)))
                nc.scalar.activation(CB[:, :], ring_bank("cb", e)[:, :], ACT.Copy).then_inc(cb.sem, 1)

            def ffn_part(s, lo, o, n):
                c = s - 1
                if n == 0:
                    for j in range(J):
                        act.wait_ge(full["yd"].sem, full["yd"].at(c, j + 1))
                        if parts(lo)[0]:
                            act.wait_ge(zc.sem, zc.at(s))
                        nc.scalar.activation(SCR[:, j, :], ring_bank("yd", j)[:, :], ACT.Copy)\
                          .then_inc(yd.sem, 1)
                if n == 2:
                    rsqrt("o", c)
                if n == 4:
                    for k in range(KM):
                        act.wait_ge(full["x1t"].sem, full["x1t"].at(c, k + 1))
                        act.wait_ge(full["up"].sem, full["up"].at(c - 1))
                        nc.scalar.activation(X1T[:, k, :], ring_bank("x1t", k)[:, :], ACT.Copy)\
                          .then_inc(x1t.sem, 1)
                if n == FS + SH:
                    act.wait_ge(full["cf"].sem, full["cf"].at(c))
                    if parts(lo)[0]:
                        act.wait_ge(full["dl"].sem, full["dl"].at(s))
                        act.wait_ge(full["ct"].sem, full["ct"].at(s))
                        act.wait_ge(blo.sem, blo.at(s))
                    nc.scalar.activation(XD[ROW_K:ROW_K + KC, :], ring_bank("cf", 0)[0:KC, :],
                                         ACT.Copy).then_inc(cff.sem, 1)
                    act.wait_ge(cff.sem, cff.at(c))
                    act.wait_ge(full["cb"].sem, full["cb"].at(c - 1))
                    nc.scalar.activation(HL[ROW_K:ROW_K + KC, o, :], XD[ROW_K:ROW_K + KC, :],
                                         ACT.Copy).then_inc(cfh.sem, 1)
                f = n - FS
                if 0 <= f < F:
                    act.wait_ge(gate_full.sem, gate_full.at(c, f + 1))
                    act.wait_ge(hid.sem, hid.at(c, f))
                    nc.scalar.activation(TG[:, :], GK[:, :], ACT.Tanh).then_inc(tg.sem, 1)
                    act.wait_ge(full["up"].sem, full["up"].at(c, f + 1))
                    act.wait_ge(hf.sem, hf.at(c, hf_done(f - 1)))
                    nc.scalar.activation(UP[:, :], ring_bank("up", f)[:, :], ACT.Copy)\
                      .then_inc(up.sem, 1)
                    if f > SH:
                        coef_take(c, f - SH)

            def prep_part(s, lo, o, n):
                c = s + 1

                def x_in(j):
                    act.wait_ge(full["xin"].sem, full["xin"].at(c, j + 1))
                    act.wait_ge(conv.sem, conv.at(c - 1))
                    nc.scalar.activation(XIN[:, j, TAPS - 1:], ring_bank("xin", j)[:, :], ACT.Copy)\
                      .then_inc(xin.sem, 1)

                def z(a):
                    act.wait_ge(full["z"].sem, full["z"].at(c, a + 1))
                    act.wait_ge(sz.sem, sz.at(c, a))
                    nc.scalar.activation(TZ[:, :], ring_bank("z", a)[:, :], ACT.Tanh)\
                      .then_inc(tz.sem, 1)
                    nc.scalar.activation(ZC[:, :], ring_bank("z", a)[:, :], ACT.Copy)\
                      .then_inc(tz.sem, 1)

                def delta(j):
                    act.wait_ge(full["dl"].sem, full["dl"].at(c, j + 1))
                    if j == 0:
                        act.wait_ge(du.sem, du.at(c - 2))
                        act.wait_ge(full["z"].sem, full["z"].at(c))
                        if parts(lo)[1]:
                            act.wait_ge(full["x1t"].sem, full["x1t"].at(s - 1))
                    nc.scalar.activation(ZB[:, j, :], ring_bank("dl", j)[:, :], ACT.Abs,
                                         bias=BDT[:, j:j + 1]).then_inc(absrelu.sem, 1)
                    nc.scalar.activation(DL[:, o, j, :], ring_bank("dl", j)[:, :], ACT.Relu,
                                         bias=BDT[:, j:j + 1]).then_inc(absrelu.sem, 1)

                if n == 0:
                    rsqrt("xa", c)
                if n == 2:
                    for k in range(KM):
                        act.wait_ge(full["xt"].sem, full["xt"].at(c, k + 1))
                        act.wait_ge(dadd.sem, dadd.at(c - 1))
                        nc.scalar.activation(XT[:, k, :], ring_bank("xt", k)[:, :], ACT.Copy)\
                          .then_inc(xt.sem, 1)
                if n == 3:
                    act.wait_ge(conv.sem, conv.at(c - 1))
                    act.wait_ge(halo.sem, halo.at(c - 1))
                    nc.scalar.activation(XIN[:, :, 0:TAPS - 1], HALO[:, o, :, :], ACT.Copy)\
                      .then_inc(halo.sem, 1)
                    x_in(0)
                    x_in(1)
                    z(0)
                if n == 4:
                    x_in(2)
                    x_in(3)
                    act.wait_ge(xin.sem, xin.at(c))
                    nc.scalar.activation(HALO[:, o, :, :], XIN[:, :, T:], ACT.Copy)\
                      .then_inc(halo.sem, 1)
                if 4 <= n < 4 + J:
                    j = n - 4
                    act.wait_ge(conv.sem, conv.at(c, TAPS * (j + 1)))
                    act.wait_ge(u_s.sem, u_s.at(c, j))
                    nc.scalar.activation(TC[:, :], SCR[:, j, :], ACT.Tanh).then_inc(tc.sem, 1)
                if n in (6, 7, 8):
                    z(n - 5)
                if n == 8:
                    act.wait_ge(full["xd"].sem, full["xd"].at(c))
                    if parts(lo)[1]:
                        act.wait_ge(cflo.sem, cflo.at(s - 1))
                    act.wait_ge(full["dl"].sem, full["dl"].at(c - 1))
                    act.wait_ge(full["ct"].sem, full["ct"].at(c - 1))
                    act.wait_ge(blo.sem, blo.at(c - 1))
                    nc.scalar.activation(XD[0:XD_ROWS, :], ring_bank("xd", 0)[0:XD_ROWS, :], ACT.Copy)\
                      .then_inc(xd.sem, 1)
                    act.wait_ge(xd.sem, xd.at(c))
                    act.wait_ge(bk_full.sem, bk_full.at(c - 2))
                    nc.scalar.activation(HL[0:ROW_B2 + NS, o, :], XD[0:ROW_B2 + NS, :], ACT.Copy)\
                      .then_inc(bhi.sem, 1)
                if n == 9:
                    act.wait_ge(full["ct"].sem, full["ct"].at(c))
                    act.wait_ge(add_c.sem, add_c.at(c - 2))
                    nc.scalar.activation(CT[:, o, :, :].rearrange("p a n -> p (a n)"),
                                         ring_bank("ct", 0)[:, 0:NT * NS], ACT.Copy).then_inc(ct.sem, 1)
                    delta(0)
                    delta(1)
                if n == 10:
                    delta(2)
                    delta(3)
                if n == 11:
                    act.wait_ge(absrelu.sem, absrelu.at(c))
                    nc.scalar.activation(ZB[:, :, :], ZB[:, :, :], ACT.Exp, scale=-1.0)\
                      .then_inc(zex.sem, 1)
                    act.wait_ge(zex.sem, zex.at(c))
                    act.wait_ge(u_s.sem, u_s.at(c))
                    nc.scalar.activation(SCR[:, :, :], ZB[:, :, :], ACT.Ln, bias=1.0)\
                      .then_inc(ln.sem, 1)

            run(act, body)

        @block.vector
        def _(dve):
            nc.vector.memset(WX[:, :, :], 0.0)
            nc.vector.memset(HALO[:, :, :, :], 0.0)
            nc.vector.memset(CARRY[:, :, :, :], 0.0)
            nc.vector.memset(COEF[:, :, :], 0.0)
            nc.vector.memset(EPST[:, :], EPS).then_inc(zeroed.sem, 1)
            dve.wait_ge(const_ld.sem, CONST_LOADS)
            dve.wait_ge(ident_made.sem, IDENT_MADE)
            dve.wait_ge(a_exp.sem, 1)
            nc.vector.tensor_scalar(WIN[:, :, DI:2 * DI], WIN[:, :, DI:2 * DI], 0.5, None, ALU.mult)
            nc.vector.tensor_scalar(WG[:, :, :, :], WG[:, :, :, :], 0.5, None, ALU.mult)
            nc.vector.tensor_scalar(CW[:, :, :], CW[:, :, :], 0.5, None, ALU.mult)
            nc.vector.tensor_scalar(CB_[:, :], CB_[:, :], 0.5, None, ALU.mult)
            nc.vector.tensor_scalar(ANEG[:, :, :], ANEG[:, :, :], -1.0, None, ALU.mult)
            nc.vector.tensor_copy(SEL[:, :], SELF)
            for j in range(J):
                last = nc.vector.tensor_scalar(DIAG[:, j, :], IDN[:, :], DSK[:, j:j + 1], None, ALU.mult)
            last.then_inc(consts.sem, 1)
            dve.wait_ge(consts.sem, 1)

            def scan_step(s, r, n, j):
                dve.wait_ge(ex.sem, ex.at(s, n * J + j + 1))
                if j % 2 == 0:
                    dve.wait_ge(bu.sem, bu.at(s, 2 * n + j // 2 + 1))
                if j == 0:
                    if n < 2:
                        dve.wait_ge(ht_full.sem, ht_full.at(s - 1, NT * (NS + n)))
                    else:
                        dve.wait_ge(ht_full.sem, ht_full.at(s, NT * n))
                    dve.wait_ge(carry.sem, carry.at(s, n))
                nc.vector.tensor_tensor_scan(H[:, n % 2, j, :], DA[:, j, :],
                                             BU[:, (2 * n + j // 2) % 4, j % 2, :],
                                             CARRY[:, r, n, j:j + 1], ALU.mult, ALU.add)\
                  .then_inc(scan.sem, 1)

            def add_state(s, r, n, a):
                dve.wait_ge(ht_full.sem, ht_full.at(s, NT * (n + 1) + a + 1))
                if n == 0:
                    dve.wait_ge(yinit.sem, yinit.at(s, a + 1))
                    dve.wait_ge(ct.sem, ct.at(s))
                else:
                    dve.wait_ge(add_c.sem, add_c.at(s, (n - 1) * NT + a + 1))
                nc.vector.scalar_tensor_tensor(YT[:, a, :], HT[(NT * (n + 1) + a) % 2][:, :],
                                               CT[:, r, a, n:n + 1], YT[:, a, :],
                                               ALU.mult, ALU.add).then_inc(add_c.sem, 1)

            def moments(w, c, a, tile):
                nc.vector.bn_stats(ST[w][:, a, :], tile).then_inc(stats[w].sem, 1)

            def moments_end(w, c):
                dve.wait_ge(stats[w].sem, stats[w].at(c, NT))
                dve.wait_ge(rstd[w].sem, rstd[w].at(c - 1))
                dve.sem_inc(waited, 1)
                for a in range(NT):
                    nc.vector.bn_aggr(MV[w][:, a, :], ST[w][:, a, :]).then_inc(stats[w].sem, 1)

            def normed(w, c, a, dst, src):
                dve.wait_ge(rstd[w].sem, rstd[w].at(c))
                nc.vector.tensor_scalar(dst, src, MV[w][:, a, 0:1], RS[w][:, a:a + 1],
                                        ALU.subtract, ALU.mult).then_inc(norm[w].sem, 1)

            def dn(a):
                return DN[a // 2][:, (a % 2) * DM:(a % 2 + 1) * DM]

            def body(s, lo, r):
                with_scan, ffn, prep = parts(lo)
                o = 1 - r
                for n in range(NS):
                    for j in range(J):
                        if with_scan:
                            scan_step(s, r, n, j)
                        if ffn:
                            ffn_part(s, o, n, 2 * j)
                        if prep:
                            prep_part(s, lo, o, n, 2 * j)
                        if with_scan and n > 0:
                            add_state(s, r, n - 1, j)
                        if ffn:
                            ffn_part(s, o, n, 2 * j + 1)
                        if prep:
                            prep_part(s, lo, o, n, 2 * j + 1)
                    if with_scan:
                        dve.wait_ge(scan.sem, scan.at(s, (n + 1) * J))
                        nc.vector.tensor_copy(CARRY[:, r, n, :], H[:, n % 2, :, T - 1])\
                          .then_inc(carry.sem, 1)
                    if prep:
                        prep_end(s, o, n)
                    if ffn:
                        ffn_end(s, lo, n)
                if ffn:
                    for a in range(NT):
                        dve.wait_ge(down.sem, down.at(s - 1))
                        moments("y", s - 1, a, dn(a))
                    moments_end("y", s - 1)
                if with_scan:
                    for a in range(NT):
                        add_state(s, r, NS - 1, a)
                if ffn:
                    for a in range(NT):
                        if prep and a == 0:
                            dve.wait_ge(dadd.sem, dadd.at(s + 1))
                        normed("y", s - 1, a, XN[:, a, :], dn(a))
                    dve.wait_ge(norm["y"].sem, norm["y"].at(s - 1))
                    nc.vector.tensor_tensor(XR[:, :, :], XR[:, :, :], XN, ALU.add)\
                      .then_inc(y_add.sem, 1)
                if with_scan:
                    for a in range(NT):
                        dve.wait_ge(add_c.sem, add_c.at(s, (NS - 1) * NT + a + 1))
                        nc.vector.tensor_tensor(YT[:, a, :], YT[:, a, :], SZ[:, r, a, :], ALU.mult)\
                          .then_inc(y_gate.sem, 1)

            def over(t):
                return t.unsqueeze(2).to_broadcast([P, NT, E])

            def route(c, i):
                if i == 2:
                    dve.wait_ge(rex.sem, rex.at(c))
                elif i > 0:
                    dve.wait_ge(rt.sem, rt.at(c, i))
                logits = DN[0][:, 0:NT * E].rearrange("p (a e) -> p a e", a=NT)
                if i == 0:
                    dve.wait_ge(rt_full.sem, rt_full.at(c))
                    last = nc.vector.tensor_reduce(RMAX, logits, X, ALU.max)
                elif i == 1:
                    last = nc.vector.tensor_tensor(RP[:, :, :], logits, over(RMAX), ALU.subtract)
                elif i == 2:
                    last = nc.vector.tensor_reduce(RSUM, RP[:, :, :], X, ALU.add)
                elif i == 3:
                    last = nc.vector.reciprocal(RINV, RSUM)
                elif i == 4:
                    last = nc.vector.tensor_tensor(RP[:, :, :], RP[:, :, :], over(RINV), ALU.mult)
                elif i in (5, 11):
                    src = RP if i == 5 else RL
                    last = nc.vector.tensor_reduce(R1, src[:, :, :], X, ALU.max)
                elif i in (6, 12):
                    src = RP if i == 6 else RL
                    last = nc.vector.tensor_tensor(RQ[:, :, :], src[:, :, :], over(R1), ALU.is_equal)
                elif i in (7, 13):
                    last = nc.vector.tensor_tensor(RQ[:, :, :], RQ[:, :, :], RANKS[:, :].unsqueeze(1).to_broadcast([P, NT, E]), ALU.mult)
                elif i in (8, 14):
                    last = nc.vector.tensor_reduce(R1, RQ[:, :, :], X, ALU.max)
                elif i in (9, 15):
                    dst = RM if i == 9 else RQ
                    last = nc.vector.tensor_tensor(dst[:, :, :], RQ[:, :, :], over(R1), ALU.is_equal)
                elif i == 10:
                    last = nc.vector.scalar_tensor_tensor(RL[:, :, :], RM[:, :, :], -4.0, RP[:, :, :],
                                                          ALU.mult, ALU.add)
                elif i == 16:
                    last = nc.vector.tensor_tensor(RM[:, :, :], RM[:, :, :], RQ[:, :, :], ALU.add)
                else:
                    at = 0 if i == 17 else ROW_K2 - ROW_K
                    last = nc.vector.tensor_tensor(COEF[:, :, at:at + E], RM[:, :, :], RP[:, :, :],
                                                   ALU.mult)
                last.then_inc(rt.sem, 1)

            def ffn_part(s, o, n, pos):
                c = s - 1
                if n == 2 and pos < NT:
                    dve.wait_ge(o_full.sem, o_full.at(c, 2 * (pos // 2) + 2))
                    moments("o", c, pos, dn(pos))
                if n == 2 and pos == NT:
                    moments_end("o", c)
                if n == 3 and pos >= 8 - NT:
                    a = pos - (8 - NT)
                    dve.wait_ge(x1_add.sem, x1_add.at(c))
                    moments("x1", c, a, XR[:, a, :])
                if n == 4 and pos < NT:
                    normed("x1", c, pos, XN[:, pos, :], XR[:, pos, :])
                if n == FS + 1:
                    first = 2 + 2 * pos
                    for i in range(first, first + 2 if pos < 7 else RT_STEPS):
                        route(c, i)

            def ffn_end(s, lo, n):
                c = s - 1
                if n == 2:
                    for a in range(NT):
                        if a == 0 and parts(lo)[0]:
                            dve.wait_ge(dadd.sem, dadd.at(s))
                        normed("o", c, a, XN[:, a, :], dn(a))
                if n == 3:
                    moments_end("x1", c)
                if n == FS:
                    route(c, 0)
                    route(c, 1)
                if n == FS + SH:
                    dve.wait_ge(cfh.sem, cfh.at(c))
                    rows = slice(ROW_K2, ROW_K2 + E)
                    nc.vector.tensor_tensor(HL[rows, 1 - lo % 2, :], XD[rows, :],
                                            HL[rows, 1 - lo % 2, :].bitcast(f32), ALU.subtract)\
                      .then_inc(cflo.sem, 1)
                f = n - FS
                if 0 <= f < F:
                    dve.wait_ge(tg.sem, tg.at(c, f + 1))
                    dve.wait_ge(down.sem, down.at(c, f))
                    nc.vector.scalar_tensor_tensor(HF[:, :], TG[:, :], 1.0, GK[:, :],
                                                   ALU.add, ALU.mult).then_inc(hid.sem, 1)

            def prep_part(s, lo, o, n, pos):
                c = s + 1
                if n == 0 and pos < NT:
                    dve.wait_ge(xa_ld.sem, xa_ld.at(c))
                    moments("xa", c, pos, XA[:, pos, :])
                if n == 0 and pos == NT:
                    moments_end("xa", c)
                if n == 1 and pos % 2 == 0:
                    normed("xa", c, pos // 2, XA[:, pos // 2, :], XA[:, pos // 2, :])
                if (n, pos) in ((4, 0), (7, 0), (8, 0), (9, 0)):
                    a = max(n - 6, 0)
                    dve.wait_ge(tz.sem, tz.at(c, 2 * (a + 1)))
                    nc.vector.scalar_tensor_tensor(SZ[:, o, a, :], TZ[:, :], 1.0, ZC[:, :],
                                                   ALU.add, ALU.mult).then_inc(sz.sem, 1)
                if 4 <= n < 4 + J and pos % 2 == 0:
                    j, k = n - 4, pos // 2
                    if k == 0:
                        dve.wait_ge(xin.sem, xin.at(c, j + 1))
                        if j == 0:
                            dve.wait_ge(halo.sem, halo.at(c, 1))
                            dve.wait_ge(zc.sem, zc.at(c - 1))
                            if parts(lo)[1]:
                                dve.wait_ge(o_full.sem, o_full.at(s - 1))
                        nc.vector.tensor_scalar(SCR[:, j, :], XIN[:, j, 0:T], CW[:, j, 0:1],
                                                CB_[:, j:j + 1], ALU.mult, ALU.add)\
                          .then_inc(conv.sem, 1)
                    else:
                        dve.wait_ge(conv.sem, conv.at(c, TAPS * j + k))
                        nc.vector.scalar_tensor_tensor(SCR[:, j, :], XIN[:, j, k:k + T],
                                                       CW[:, j, k:k + 1], SCR[:, j, :],
                                                       ALU.mult, ALU.add).then_inc(conv.sem, 1)
                if n == 12:
                    j = pos // 2
                    if pos % 2 == 0:
                        dve.wait_ge(ln.sem, ln.at(c))
                        nc.vector.tensor_tensor(DL[:, o, j, :], DL[:, o, j, :], SCR[:, j, :], ALU.add)\
                          .then_inc(lsum.sem, 1)
                    else:
                        dve.wait_ge(lsum.sem, lsum.at(c, j + 1))
                        nc.vector.tensor_scalar(SCR[:, j, :], ZB[:, j, :], 1.0, -1.0,
                                                ALU.add, ALU.add).then_inc(w1.sem, 1)

            def prep_end(s, o, n):
                c = s + 1
                if 4 <= n < 4 + J:
                    j = n - 4
                    dve.wait_ge(tc.sem, tc.at(c, j + 1))
                    if j == 0:
                        dve.wait_ge(ht_full.sem, ht_full.at(s, NT))
                        dve.wait_ge(du.sem, du.at(s))
                    nc.vector.scalar_tensor_tensor(U[:, j, :], TC[:, :], 1.0, SCR[:, j, :],
                                                   ALU.add, ALU.mult).then_inc(u_s.sem, 1)
                if n == 8:
                    dve.wait_ge(bhi.sem, bhi.at(c))
                    rows = slice(ROW_B2, ROW_B2 + NS)
                    nc.vector.tensor_tensor(HL[rows, o, :], XD[rows, :],
                                            HL[rows, o, :].bitcast(f32), ALU.subtract)\
                      .then_inc(blo.sem, 1)

            run(dve, body)

        @block.gpsimd
        def _(pool):
            nc.gpsimd.memset(IDN[:, :], 0.0).then_inc(ident_made.sem, 1)
            nc.gpsimd.memset(SELF, 0.0).then_inc(ident_made.sem, 1)
            pool.wait_ge(ident_made.sem, 2)
            nc.gpsimd.affine_select(out=IDN[:, :], in_=IDN[:, :], compare_op=ALU.not_equal, fill=1.0,
                                    base=0, pattern=[[-1, P]], channel_multiplier=1)\
              .then_inc(ident_made.sem, 1)
            for q in range(P // 32):
                pool.wait_ge(ident_made.sem, 3 + q)
                nc.gpsimd.affine_select(out=SELF, in_=SELF, compare_op=ALU.not_equal,
                                        fill=1.0, base=-32 * q, pattern=[[-1, NS]],
                                        channel_multiplier=1).then_inc(ident_made.sem, 1)
            for e in range(E):
                nc.gpsimd.memset(RANKS[:, e:e + 1], float(E - e)).then_inc(ident_made.sem, 1)

            def inflow(s, n):
                pool.wait_ge(bb.sem, bb.at(s, n + 1))
                for h in range(2):
                    if n == 0:
                        pool.wait_ge(du.sem, du.at(s, 2 * h + 2))
                    if n < 2:
                        pool.wait_ge(scan.sem, scan.at(s - 1, (n + NS - 2) * J + 2 * h + 2))
                    else:
                        pool.wait_ge(scan.sem, scan.at(s, (n - 2) * J + 2 * h + 2))
                    nc.gpsimd.tensor_tensor(BU[:, (2 * n + h) % 4, :, :], DU[:, 2 * h:2 * h + 2, :],
                                            BB[:, n % 2, :].unsqueeze(1).to_broadcast([P, 2, T]),
                                            ALU.mult).then_inc(bu.sem, 1)

            def body(s, lo, r):
                with_scan, ffn, prep = parts(lo)
                o = 1 - r
                if with_scan:
                    inflow(s, 0)
                for n in range(NS):
                    if with_scan and n + 1 < NS:
                        inflow(s, n + 1)
                    if ffn and n == 2:
                        pool.wait_ge(norm["o"].sem, norm["o"].at(s - 1))
                        pool.wait_ge(xr_ld.sem, xr_ld.at(s - 1))
                        nc.gpsimd.tensor_tensor(XR[:, :, :], XR[:, :, :], XN, ALU.add)\
                          .then_inc(x1_add.sem, 1)
                    if prep:
                        prep_part(s + 1, s, o, n)
                    f = n - FS
                    if ffn and 0 <= f < F:
                        hidden(s - 1, f)

            def hidden(c, f):
                pool.wait_ge(hid.sem, hid.at(c, f + 1))
                pool.wait_ge(up.sem, up.at(c, f + 1))
                nc.gpsimd.tensor_tensor(HF[:, :], HF[:, :], UP[:, :], ALU.mult).then_inc(hf.sem, 1)
                if f >= SH:
                    pool.wait_ge(hf.sem, hf.at(c, hf_done(f) - 1))
                    pool.wait_ge(cb.sem, cb.at(c, f - SH + 1))
                    nc.gpsimd.tensor_tensor(HF[:, :], HF[:, :], CB[:, :], ALU.mult)\
                      .then_inc(hf.sem, 1)

            def prep_part(c, s, o, n):
                if n in (12, 13):
                    for j in (2 * (n - 12), 2 * (n - 12) + 1):
                        pool.wait_ge(w1.sem, w1.at(c, j + 1))
                        nc.gpsimd.tensor_tensor(ZB[:, j, :], ZB[:, j, :], SCR[:, j, :], ALU.subtract)\
                          .then_inc(zc.sem, 1)
                if n in (14, 15):
                    for j in (2 * (n - 14), 2 * (n - 14) + 1):
                        pool.wait_ge(zc.sem, zc.at(c, j + 1))
                        pool.wait_ge(lsum.sem, lsum.at(c, j + 1))
                        nc.gpsimd.tensor_tensor(DL[:, o, j, :], DL[:, o, j, :], ZB[:, j, :], ALU.add)\
                          .then_inc(dadd.sem, 1)
                if n == 15:
                    for j in range(J):
                        pool.wait_ge(dadd.sem, dadd.at(c, j + 1))
                        pool.wait_ge(u_s.sem, u_s.at(c))
                        if j == 0:
                            pool.wait_ge(bu.sem, bu.at(s))
                        nc.gpsimd.tensor_tensor(DU[:, j, :], DL[:, o, j, :], U[:, j, :], ALU.mult)\
                          .then_inc(du.sem, 1)

            run(pool, body)


_INS = ["L0_attn_x", "L0_attn_W_in", "L0_attn_conv_w", "L0_attn_conv_b", "L0_attn_W_xproj",
        "L0_attn_W_dt", "L0_attn_b_dt", "L0_attn_A_log", "L0_attn_D_skip", "L0_attn_W_out",
        "L0_ffn_router", "L0_ffn_experts_gate", "L0_ffn_experts_up", "L0_ffn_experts_down",
        "L0_ffn_shared_gate", "L0_ffn_shared_up", "L0_ffn_shared_down"]


def kernel(**inputs):
    import numpy as _np
    import concourse.bacc as _bacc
    from concourse import mybir as _mybir
    from concourse.bass_utils import run_bass_kernel_spmd as _run

    nc = _bacc.Bacc("TRN2", target_bir_lowering=False, num_devices=1)
    arrays, args = {}, []
    for name in _INS:
        a = _np.ascontiguousarray(inputs[name])
        arrays[name + "_in"] = a
        args.append(nc.dram_tensor(name + "_in", a.shape, _mybir.dt.from_np(a.dtype),
                                   kind="ExternalInput").ap())
    shape = inputs["L0_attn_x"].shape
    args.append(nc.dram_tensor("out", shape, _mybir.dt.float32, kind="ExternalOutput").ap())
    mamba_moe_kernel(nc, *args)
    r = _run(nc, [arrays], core_ids=[0])
    return r.results[0]["out"]
```

```python
from contextlib import ExitStack

import concourse.bass as bass
from concourse import mybir


class Stage:

    def __init__(self, sem, per):
        self.sem, self.per = sem, per

    def at(self, chunk, k=None):
        value = chunk * self.per + (self.per if k is None else k)
        return max(value, 0) if isinstance(value, int) else value


def mamba_moe_kernel(nc, x, w_in, conv_w, conv_b, w_xproj, w_dt, b_dt, a_log, d_skip, w_out,
                     router, e_gate, e_up, e_down, s_gate, s_up, s_down, out):
    f32, f32r = mybir.dt.float32, mybir.dt.float32r
    ALU, ACT, X = mybir.AluOpType, mybir.ActivationFunctionType, mybir.AxisListType.X
    P = 128
    BATCH, LENGTH, DM = x.shape
    DI, TAPS = conv_w.shape[0], conv_w.shape[2]
    NS = a_log.shape[1]
    RANK = w_dt.shape[0]
    E = router.shape[1]
    T = 512
    NT = T // P
    KM = DM // P
    J = DI // P
    SH = s_gate.shape[1] // P
    F = SH + E
    CHUNKS = BATCH * LENGTH // T
    EPS = 1e-5
    ROW_B, ROW_B2, ROW_DT, ROW_C = 0, 32, 64, 96
    XD_ROWS = ROW_C + NS
    ROW_K, ROW_K2 = 64, 96
    KC = ROW_B2 + E

    with ExitStack() as ctx:
        def sb(name, shape, dt=f32):
            return ctx.enter_context(nc.sbuf_tensor(name, shape, dt))

        def ps(name):
            return ctx.enter_context(nc.psum_tensor(name, [P, 512], f32))

        def stage(name, per):
            return Stage(ctx.enter_context(nc.semaphore(name)), per)

        WIN = sb("w_in_sb", [P, KM, 2 * DI])
        WG = sb("w_gate_sb", [P, KM, F, P])
        WU = sb("w_up_sb", [P, KM, F, P])
        WD = sb("w_down_sb", [P, F, DM])
        WO = sb("w_out_sb", [P, J, DM])
        WX = sb("w_xproj_sb", [P, J, XD_ROWS])
        WDT = sb("w_dt_sb", [P, DI])
        WR = sb("router_sb", [P, KM, E])
        CW = sb("conv_w_sb", [P, J, TAPS])
        CB_ = sb("conv_b_sb", [P, J])
        BDT = sb("b_dt_sb", [P, J])
        DSK = sb("d_skip_sb", [P, J])
        ANEG = sb("a_neg", [P, J, NS])
        EPST = sb("eps", [P, 1])
        IDN = sb("ident", [P, P])
        DIAG = sb("diag_d", [P, J, P])
        SEL = sb("sel", [P, NS], f32r)
        RANKS = sb("ranks", [P, E])
        XA = sb("xa", [P, NT, DM])
        ZB = sb("z_buf", [P, J, T])
        XN = ZB[:, 0:2, :].rearrange("p j t -> p (j t)").rearrange("p (a d) -> p a d", a=NT)
        XT = ZB[:, 2:4, :]
        SCR = sb("scratch", [P, J, T])
        XIN = sb("xin", [P, J, T + TAPS - 1])
        HALO = sb("halo", [P, BATCH, J, TAPS - 1])
        U = sb("u", [P, J, T])
        TC = sb("tanh_conv", [P, T])
        TZ = sb("tanh_z", [P, T])
        ZC = sb("z_copy", [P, T])
        SZ = sb("silu_z", [P, 2, NT, DI])
        DL = sb("delta", [P, 2, J, T])
        DU = sb("delta_u", [P, J, T])
        XD = sb("x_dbl", [P, T])
        HL = sb("hi_lo", [P, 2, T], f32r)
        CT = sb("c_t", [P, 2, NT, NS])
        BB = sb("b_rows", [P, 2, T])
        DA = sb("d_a", [P, J, T])
        BU = sb("d_bu", [P, 4, 2, T])
        H = sb("h", [P, 2, J, T])
        CARRY = sb("carry", [P, BATCH, NS, J])
        YT = sb("y_t", [P, NT, DI])
        XR = sb("xr", [P, NT, DM])
        X1T = sb("x1_t", [P, KM, T])
        TG = sb("tanh_gate", [P, T])
        HF = sb("hidden", [P, T])
        UP = sb("up", [P, T])
        CB = sb("coef_rows", [P, T])
        ST = {w: sb(f"stats_{w}", [P, NT, 6]) for w in ("xa", "o")}
        ST["x1"] = ST["y"] = ST["o"]
        MV = {w: sb(f"mean_var_{w}", [P, NT, 2]) for w in ("xa", "o", "x1", "y")}
        RS = {w: sb(f"rstd_{w}", [P, NT]) for w in ("xa", "o", "x1", "y")}
        R_SMALL = sb("r_small", [P, 4, NT])
        RMAX, RSUM, RINV, R1 = (R_SMALL[:, i, :] for i in range(4))
        RP = sb("r_prob", [P, NT, E])
        RQ = sb("r_equal", [P, NT, E])
        RM = sb("r_mask", [P, NT, E])
        RL = sb("r_left", [P, NT, E])
        SELF = RQ[:, :, :].rearrange("p a e -> p (a e)")[:, 0:NS]
        COEF = sb("coef", [P, NT, KC])

        HT = [ps("ht0"), ps("ht1")]
        DN = [ps("dn0"), ps("dn1")]
        BK = ps("b_bank")
        GK = ps("gate_bank")
        RING = [ps("ring0"), ps("ring1")]

        const_ld, xa_ld = stage("const_ld", 0), stage("xa_ld", 16)
        xr_ld, out_st = stage("xr_ld", 16), stage("out_st", 16)
        zeroed, ident_made, consts = stage("zeroed", 0), stage("ident_made", 0), stage("consts", 0)
        a_exp = stage("a_exp", 0)
        bk_full, ht_full = stage("bk_full", NS), stage("ht_full", NT * (NS + 1))
        full = {w: stage(f"{w}_full", n) for w, n in dict(
            yd=J, xt=KM, xin=J, z=NT, x1t=KM, up=F, cf=1, cb=E, xd=1, ct=1, dl=J).items()}
        o_full, rt_full = stage("o_full", NT), stage("rt_full", 1)
        gate_full, down = stage("gate_full", F), stage("down", F)
        bb, ex = stage("bb", NS), stage("ex", NS * J)
        yd, yinit, xt = stage("yd", J), stage("yinit", NT), stage("xt", KM)
        rstd = {w: stage(f"rstd_{w}_s", 2) for w in ("xa", "o", "x1", "y")}
        halo, xin, tz = stage("halo_s", 2), stage("xin_s", J), stage("tz_s", 2 * NT)
        x1t, tc, tg, up = stage("x1t_s", KM), stage("tc_s", J), stage("tg_s", F), stage("up_s", F)
        rex, cff, cfh, cb = stage("rex", 1), stage("cff", 1), stage("cfh", 1), stage("cb_s", E)
        xd, bhi, ct = stage("xd_s", 1), stage("bhi", 1), stage("ct_s", 1)
        absrelu, zex, ln = stage("absrelu", 2 * J), stage("zex", 1), stage("ln", 1)
        scan, add_c, carry = stage("scan", NS * J), stage("add_c", NS * NT), stage("carry_s", NS)
        stats = {w: stage(f"stats_{w}_s", 2 * NT) for w in ("xa", "o", "x1", "y")}
        norm = {w: stage(f"norm_{w}", NT) for w in ("xa", "o", "x1", "y")}
        y_add, y_gate = stage("y_add", 1), stage("y_gate", NT)
        conv, u_s, sz = stage("conv", J * TAPS), stage("u_s", J), stage("sz", NT)
        RT_STEPS = 19
        rt = stage("rt", RT_STEPS)
        hid, cflo, blo = stage("hid", F), stage("cflo", 1), stage("blo", 1)
        lsum, w1 = stage("lsum", J), stage("w1", J)
        waited = ctx.enter_context(nc.semaphore("waited"))
        bu, x1_add = stage("bu", 2 * NS), stage("x1_add", 2)
        hf = stage("hf", SH + 2 * E)
        zc, dadd, du = stage("zc", J), stage("dadd", J), stage("du", J)

        def hf_done(k):
            return k + 1 if k < SH else SH + 2 * (k + 1 - SH)

        def up_used(k):
            return k + 1 if k < SH else hf_done(k) - 1

        FS = 5
        RING_USE = [("yd", -1, j) for j in range(J)]
        RING_USE += [("xt", 1, k) for k in range(KM)] + [("xin", 1, j) for j in range(J)]
        RING_USE += [("z", 1, 0), ("z", 1, 1)] + [("x1t", -1, k) for k in range(KM)]
        RING_USE += [("up", -1, 0), ("up", -1, 1), ("z", 1, 2)]
        RING_USE += [("cf", -1, 0), ("up", -1, 2), ("z", 1, 3), ("xd", 1, 0), ("cb", -1, 0)]
        RING_USE += [("up", -1, 3), ("cb", -1, 1), ("ct", 1, 0), ("dl", 1, 0), ("dl", 1, 1)]
        RING_USE += [("up", -1, 4), ("cb", -1, 2), ("dl", 1, 2), ("dl", 1, 3)]
        for k in range(5, F):
            RING_USE += [("up", -1, k), ("cb", -1, k - SH)]
        ring_free = {"yd": (yd, 1), "xt": (xt, 1), "xin": (xin, 1), "z": (tz, 2), "x1t": (x1t, 1),
                     "up": (up, 1), "cf": (cff, 1), "cb": (cb, 1), "xd": (xd, 1), "ct": (ct, 1),
                     "dl": (absrelu, 2)}

        def ring_bank(what, k):
            at = next(i for i, use in enumerate(RING_USE) if use[0] == what and use[2] == k)
            return RING[at % 2]

        def ring_user_before(s, lo, what, k):
            at = next(i for i, use in enumerate(RING_USE) if use[0] == what and use[2] == k)
            back, parity = 0, at % 2
            while lo - back >= -1:
                at -= 1
                if at < 0:
                    at, back = len(RING_USE) - 1, back + 1
                before, part, kb = RING_USE[at]
                if at % 2 == parity and 0 <= lo - back + part < CHUNKS:
                    freed, per = ring_free[before]
                    return freed.sem, freed.at(s - back + part, per * (kb + 1))
            return yd.sem, 0

        bodies_before = [-1, 0, 1]
        loop_first, loop_last = 2, CHUNKS - 3
        bodies_after = [CHUNKS - 2, CHUNKS - 1, CHUNKS]

        def run(engine, body):
            for s in bodies_before:
                body(s, s, s % 2)
            with engine.Fori(0, (loop_last - loop_first + 1) // 2) as i:
                for r in range(2):
                    body(2 * i + loop_first + r, loop_first + r, r)
            for s in bodies_after:
                body(s, s, s % 2)

        def parts(lo):
            return 0 <= lo < CHUNKS, 0 <= lo - 1 < CHUNKS, 0 <= lo + 1 < CHUNKS

        def tokens(dram, batch, index):
            return dram[batch, bass.ds(index * T, T), :].rearrange("(a p) d -> p a d", p=P)

        block = ctx.enter_context(nc.Block())

        @block.sync
        def _(sp):
            loads = [
                (WIN[:, :, :], w_in.rearrange("(k p) c -> p k c", p=P)),
                (CW[:, :, :], conv_w.rearrange("(j p) o k -> p j (o k)", p=P)),
                (CB_[:, :], conv_b.rearrange("(j p) -> p j", p=P)),
                (BDT[:, :], b_dt.rearrange("(j p) -> p j", p=P)),
                (DSK[:, :], d_skip.rearrange("(j p) -> p j", p=P)),
                (ANEG[:, :, :], a_log.rearrange("(j p) n -> p j n", p=P)),
                (WDT[ROW_DT:ROW_DT + RANK, :], w_dt),
                (WO[:, :, :], w_out.rearrange("(j p) c -> p j c", p=P)),
                (WR[:, :, :], router.rearrange("(k p) e -> p k e", p=P)),
            ]
            for k in range(KM):
                rows = slice(k * P, (k + 1) * P)
                for dst, shared, experts in ((WG, s_gate, e_gate), (WU, s_up, e_up)):
                    loads.append((dst[:, k, 0:SH, :], shared[rows, :].rearrange("p (g f) -> p g f", g=SH)))
                    loads.append((dst[:, k, SH:F, :], experts[:, rows, :].rearrange("e p f -> p e f")))
            loads.append((WD[:, 0:SH, :], s_down.rearrange("(g p) c -> p g c", p=P)))
            loads.append((WD[:, SH:F, :], e_down.rearrange("e p c -> p e c")))
            sp.dma_start(XA[:, :, :], tokens(x, 0, 0)).then_inc(xa_ld.sem, 16)
            with nc.allow_non_contiguous_dma(reason="512 values each"):
                for dst, src in loads:
                    sp.dma_start(dst, src).then_inc(const_ld.sem, 16)
            sp.wait_ge(zeroed.sem, 1)
            wx = w_xproj.rearrange("(j p) c -> p j c", p=P)
            for row, col in ((ROW_B, RANK), (ROW_B2, RANK), (ROW_DT, 0), (ROW_C, RANK + NS)):
                width = RANK if row == ROW_DT else NS
                sp.dma_start(WX[:, :, row:row + width], wx[:, :, col:col + width])\
                  .then_inc(const_ld.sem, 16)

            def body(s, lo, r):
                _, ffn, _ = parts(lo)
                if ffn:
                    sp.wait_ge(out_st.sem, out_st.at(s - 2))
                    sp.dma_start(XR[:, :, :], tokens(x, 1 - r, (s - 1 - (1 - r)) // 2))\
                      .then_inc(xr_ld.sem, 16)
                if 0 <= lo + 2 < CHUNKS:
                    sp.wait_ge(full["xt"].sem, full["xt"].at(s + 1))
                    sp.dma_start(XA[:, :, :], tokens(x, r, (s + 2 - r) // 2)).then_inc(xa_ld.sem, 16)
                if ffn:
                    sp.wait_ge(y_add.sem, y_add.at(s - 1))
                    sp.dma_start(tokens(out, 1 - r, (s - 1 - (1 - r)) // 2), XR[:, :, :])\
                      .then_inc(out_st.sem, 16)

            for s in bodies_before:
                body(s, s, s % 2)
            with sp.Fori(0, (loop_last - loop_first + 1) // 2) as i:
                for r in range(2):
                    s = 2 * i + loop_first + r
                    sp.wait_ge(out_st.sem, out_st.at(s - 2))
                    sp.dma_start(XR[:, :, :], tokens(x, 1 - r, i + (loop_first + 2 * r - 2) // 2))\
                      .then_inc(xr_ld.sem, 16)
                    sp.wait_ge(full["xt"].sem, full["xt"].at(s + 1))
                    sp.dma_start(XA[:, :, :], tokens(x, r, i + (loop_first + 2) // 2)).then_inc(xa_ld.sem, 16)
                    sp.wait_ge(y_add.sem, y_add.at(s - 1))
                    sp.dma_start(tokens(out, 1 - r, i + (loop_first + 2 * r - 2) // 2), XR[:, :, :])\
                      .then_inc(out_st.sem, 16)
            for s in bodies_after:
                body(s, s, s % 2)
            sp.wait_ge(out_st.sem, out_st.at(CHUNKS - 1))

        IDENT_MADE = 3 + P // 32 + E
        CONST_LOADS = (9 + 4 * KM + 2 + 4) * 16

        @block.tensor
        def _(pe):
            pe.wait_ge(consts.sem, 1)
            pe.wait_ge(const_ld.sem, CONST_LOADS)
            pe.wait_ge(ident_made.sem, IDENT_MADE)

            def b_rows(s, r, n):
                pe.wait_ge(bb.sem, bb.at(s, n))
                nc.tensor.matmul(BK[:, :], SEL[0:ROW_B2 + NS, n:n + 1].to_broadcast([ROW_B2 + NS, P]),
                                 HL[0:ROW_B2 + NS, r, :], start=True, stop=True)\
                  .then_inc(bk_full.sem, 1)

            def ht_user_before(s, q):
                if q < 2:
                    return add_c.sem, add_c.at(s - 1, NS * NT - 1 + q)
                if q < NT + 2:
                    return yinit.sem, yinit.at(s, q - 1)
                return add_c.sem, add_c.at(s, q - NT - 1)

            def body(s, lo, r):
                with_scan, ffn, prep = parts(lo)
                o = 1 - r
                if with_scan:
                    pe.wait_ge(blo.sem, blo.at(s))
                    b_rows(s, r, 0)
                    b_rows(s, r, 1)
                for n in range(NS):
                    if with_scan and n + 2 < NS:
                        b_rows(s, r, n + 2)
                    for a in range(NT):
                        if with_scan and n == 0:
                            transpose_du(s, a)
                        elif with_scan:
                            transpose_state(s, n - 1, a)
                        if a > 0:
                            if ffn:
                                ffn_part(s, lo, o, n, a)
                            if prep:
                                prep_part(s, lo, o, n, a)
                        if ffn and a == NT - 1 and n == FS + SH:
                            coef_rows(s, lo, o, 0)
                        if ffn and a == NT - 1 and 0 <= n - FS - 1 < F:
                            down_part(s - 1, n - FS - 1)
                if with_scan:
                    for a in range(NT):
                        transpose_state(s, NS - 1, a)

            def transpose_du(s, a):
                pe.wait_ge(*ht_user_before(s, a))
                for j in range(J):
                    last = nc.tensor.matmul(HT[a % 2][:, j * P:(j + 1) * P],
                                            U[:, j, a * P:(a + 1) * P], DIAG[:, j, :],
                                            start=True, stop=True)
                last.then_inc(ht_full.sem, 1)

            def transpose_state(s, n, a):
                if a == 0:
                    pe.wait_ge(scan.sem, scan.at(s, (n + 1) * J))
                q = NT * (n + 1) + a
                pe.wait_ge(*ht_user_before(s, q))
                for j in range(J):
                    last = nc.tensor.transpose(HT[q % 2][:, j * P:(j + 1) * P],
                                               H[:, n % 2, j, a * P:(a + 1) * P], IDN[:, :])
                last.then_inc(ht_full.sem, 1)

            def project_out(c, a):
                for j in range(J):
                    last = nc.tensor.matmul(DN[a // 2][:, (a % 2) * DM:(a % 2 + 1) * DM],
                                            SCR[:, j, a * P:(a + 1) * P], WO[:, j, :],
                                            start=(j == 0), stop=(j == J - 1))
                last.then_inc(o_full.sem, 1)

            def ffn_part(s, lo, o, n, at):
                c = s - 1
                if (n, at) == (0, 1):
                    pe.wait_ge(y_gate.sem, y_gate.at(c))
                    for j in range(J):
                        pe.wait_ge(*ring_user_before(s, lo, "yd", j))
                        bank = ring_bank("yd", j)
                        for a in range(NT):
                            last = nc.tensor.transpose(bank[:, a * P:(a + 1) * P],
                                                       YT[:, a, j * P:(j + 1) * P], IDN[:, :])
                        last.then_inc(full["yd"].sem, 1)
                if (n, at) == (0, 3):
                    pe.wait_ge(yd.sem, yd.at(c))
                    pe.wait_ge(norm["y"].sem, norm["y"].at(c - 1))
                    project_out(c, 0)
                    project_out(c, 1)
                if n == 1 and at < 3:
                    project_out(c, at + 1)
                if (n, at) == (4, 3):
                    pe.wait_ge(norm["x1"].sem, norm["x1"].at(c))
                    for k in range(KM):
                        pe.wait_ge(*ring_user_before(s, lo, "x1t", k))
                        bank = ring_bank("x1t", k)
                        for a in range(NT):
                            last = nc.tensor.transpose(bank[:, a * P:(a + 1) * P],
                                                       XN[:, a, k * P:(k + 1) * P], IDN[:, :])
                        last.then_inc(full["x1t"].sem, 1)
                if (n, at) == (FS, 1):
                    pe.wait_ge(x1t.sem, x1t.at(c))
                    pe.wait_ge(norm["o"].sem, norm["o"].at(c))
                    for a in range(NT):
                        for k in range(KM):
                            last = nc.tensor.matmul(DN[0][:, a * E:(a + 1) * E],
                                                    X1T[:, k, a * P:(a + 1) * P], WR[:, k, :],
                                                    start=(k == 0), stop=(k == KM - 1))
                    last.then_inc(rt_full.sem, 1)
                if (n, at) == (FS + SH, 1):
                    pe.wait_ge(rt.sem, rt.at(c))
                    pe.wait_ge(*ring_user_before(s, lo, "cf", 0))
                    bank = ring_bank("cf", 0)
                    for a in range(NT):
                        last = nc.tensor.matmul(bank[0:KC, a * P:(a + 1) * P], COEF[:, a, :],
                                                IDN[:, :], start=True, stop=True)
                    last.then_inc(full["cf"].sem, 1)
                f = n - FS
                if 0 <= f < F and at == 1:
                    pe.wait_ge(hid.sem, hid.at(c, f))
                    for k in range(KM):
                        last = nc.tensor.matmul(GK[:, :], WG[:, k, f, :], X1T[:, k, :],
                                                start=(k == 0), stop=(k == KM - 1))
                    last.then_inc(gate_full.sem, 1)
                if 0 <= f < F and at == 2:
                    pe.wait_ge(*ring_user_before(s, lo, "up", f))
                    bank = ring_bank("up", f)
                    for k in range(KM):
                        last = nc.tensor.matmul(bank[:, :], WU[:, k, f, :], X1T[:, k, :],
                                                start=(k == 0), stop=(k == KM - 1))
                    last.then_inc(full["up"].sem, 1)
                if SH < f < F and at == 3:
                    coef_rows(s, lo, o, f - SH)

            def coef_rows(s, lo, o, e):
                pe.wait_ge(cflo.sem, cflo.at(s - 1))
                pe.wait_ge(*ring_user_before(s, lo, "cb", e))
                nc.tensor.matmul(ring_bank("cb", e)[:, :],
                                 SEL[ROW_K:ROW_K + KC, e:e + 1].to_broadcast([KC, P]),
                                 HL[ROW_K:ROW_K + KC, o, :], start=True, stop=True)\
                  .then_inc(full["cb"].sem, 1)

            def down_part(c, f):
                pe.wait_ge(hf.sem, hf.at(c, hf_done(f)))
                if f == 0:
                    pe.wait_ge(rt.sem, rt.at(c, 2))
                for a in range(NT):
                    last = nc.tensor.matmul(DN[a // 2][:, (a % 2) * DM:(a % 2 + 1) * DM],
                                            HF[:, a * P:(a + 1) * P], WD[:, f, :],
                                            start=(f == 0 and a % 2 == 0), stop=(f == F - 1),
                                            skip_group_check=True)
                last.then_inc(down.sem, 1)

            def prep_part(s, lo, o, n, at):
                c = s + 1

                def x_in(j):
                    pe.wait_ge(*ring_user_before(s, lo, "xin", j))
                    for k in range(KM):
                        last = nc.tensor.matmul(ring_bank("xin", j)[:, :], WIN[:, k, j * P:(j + 1) * P],
                                                XT[:, k, :], start=(k == 0), stop=(k == KM - 1))
                    last.then_inc(full["xin"].sem, 1)

                def z(a):
                    pe.wait_ge(*ring_user_before(s, lo, "z", a))
                    for k in range(KM):
                        last = nc.tensor.matmul(ring_bank("z", a)[:, :], XT[:, k, a * P:(a + 1) * P],
                                                WIN[:, k, DI:2 * DI], start=(k == 0), stop=(k == KM - 1))
                    last.then_inc(full["z"].sem, 1)

                def delta(j):
                    pe.wait_ge(*ring_user_before(s, lo, "dl", j))
                    nc.tensor.matmul(ring_bank("dl", j)[:, :], WDT[ROW_DT:ROW_DT + RANK, j * P:(j + 1) * P],
                                     XD[ROW_DT:ROW_DT + RANK, :], start=True, stop=True)\
                      .then_inc(full["dl"].sem, 1)

                if (n, at) == (2, 1):
                    pe.wait_ge(norm["xa"].sem, norm["xa"].at(c))
                    for k in range(KM):
                        pe.wait_ge(*ring_user_before(s, lo, "xt", k))
                        for a in range(NT):
                            last = nc.tensor.transpose(ring_bank("xt", k)[:, a * P:(a + 1) * P],
                                                       XA[:, a, k * P:(k + 1) * P], IDN[:, :])
                        last.then_inc(full["xt"].sem, 1)
                if (n, at) == (2, 3):
                    pe.wait_ge(xt.sem, xt.at(c))
                    x_in(0)
                    x_in(1)
                if n == 3 and at < 3:
                    x_in(at + 1)
                if (n, at) == (3, 3):
                    z(0)
                if (n, at) == (4, 1):
                    z(1)
                if n in (6, 7) and at == 3:
                    z(n - 4)
                if (n, at) == (7, 3):
                    pe.wait_ge(u_s.sem, u_s.at(c))
                    pe.wait_ge(*ring_user_before(s, lo, "xd", 0))
                    for j in range(J):
                        last = nc.tensor.matmul(ring_bank("xd", 0)[0:XD_ROWS, :], WX[:, j, :], U[:, j, :],
                                                start=(j == 0), stop=(j == J - 1))
                    last.then_inc(full["xd"].sem, 1)
                if (n, at) == (8, 3):
                    pe.wait_ge(xd.sem, xd.at(c))
                    pe.wait_ge(*ring_user_before(s, lo, "ct", 0))
                    for a in range(NT):
                        last = nc.tensor.matmul(ring_bank("ct", 0)[:, a * NS:(a + 1) * NS],
                                                XD[ROW_C:ROW_C + NS, a * P:(a + 1) * P],
                                                IDN[ROW_C:ROW_C + NS, ROW_C:ROW_C + NS],
                                                start=True, stop=True)
                    last.then_inc(full["ct"].sem, 1)
                    delta(0)
                    delta(1)
                if (n, at) == (9, 3):
                    delta(2)
                    delta(3)

            run(pe, body)

        @block.scalar
        def _(act):
            act.wait_ge(const_ld.sem, CONST_LOADS)
            nc.scalar.activation(ANEG[:, :, :], ANEG[:, :, :], ACT.Exp).then_inc(a_exp.sem, 1)
            act.wait_ge(consts.sem, 1)

            def b_take(s, n):
                act.wait_ge(bk_full.sem, bk_full.at(s, n + 1))
                if n < 2:
                    act.wait_ge(bu.sem, bu.at(s - 1, 2 * (n + NS - 2) + 2))
                else:
                    act.wait_ge(bu.sem, bu.at(s, 2 * (n - 2) + 2))
                nc.scalar.activation(BB[:, n % 2, :], BK[:, :], ACT.Copy).then_inc(bb.sem, 1)

            def decay(s, r, n, j):
                if n == 0:
                    act.wait_ge(scan.sem, scan.at(s - 1, (NS - 1) * J + j + 1))
                    act.wait_ge(dadd.sem, dadd.at(s, j + 1))
                else:
                    act.wait_ge(scan.sem, scan.at(s, (n - 1) * J + j + 1))
                nc.scalar.activation(DA[:, j, :], DL[:, r, j, :], ACT.Exp,
                                     scale=ANEG[:, j, n:n + 1]).then_inc(ex.sem, 1)

            def rsqrt(w, c):
                act.wait_ge(stats[w].sem, stats[w].at(c))
                act.wait_ge(norm[w].sem, norm[w].at(c - 1))
                nc.scalar.activation(RS[w][:, :], MV[w][:, :, 1], ACT.Ln, bias=EPST[:, 0:1])\
                  .then_inc(rstd[w].sem, 1)
                act.wait_ge(rstd[w].sem, rstd[w].at(c, 1))
                nc.scalar.activation(RS[w][:, :], RS[w][:, :], ACT.Exp, scale=-0.5)\
                  .then_inc(rstd[w].sem, 1)

            def body(s, lo, r):
                with_scan, ffn, prep = parts(lo)
                o = 1 - r
                if with_scan:
                    b_take(s, 0)
                    b_take(s, 1)
                    for j in range(J):
                        decay(s, r, 0, j)
                for n in range(NS):
                    if with_scan and n + 2 < NS:
                        b_take(s, n + 2)
                    for at in range(J):
                        if with_scan and n + 1 < NS:
                            decay(s, r, n + 1, at)
                        if ffn:
                            ffn_part(s, lo, o, n, at)
                        if with_scan and n == 0 and at == 2:
                            for a in range(NT):
                                act.wait_ge(ht_full.sem, ht_full.at(s, a + 1))
                                act.wait_ge(full["yd"].sem, full["yd"].at(s - 1))
                                nc.scalar.activation(YT[:, a, :], HT[a % 2][:, :], ACT.Copy)\
                                  .then_inc(yinit.sem, 1)
                        if prep:
                            prep_part(s, lo, o, n, at)
                        if ffn and n == FS + SH and at == 3:
                            coef_take(s - 1, 0)
                if ffn:
                    rsqrt("y", s - 1)

            def coef_take(c, e):
                act.wait_ge(full["cb"].sem, full["cb"].at(c, e + 1))
                k = SH + e
                act.wait_ge(hf.sem, hf.at(c, hf_done(k - 1)))
                nc.scalar.activation(CB[:, :], ring_bank("cb", e)[:, :], ACT.Copy).then_inc(cb.sem, 1)

            def ffn_part(s, lo, o, n, at):
                c = s - 1
                if n == 0 and at < 2:
                    for j in (2 * at, 2 * at + 1):
                        act.wait_ge(full["yd"].sem, full["yd"].at(c, j + 1))
                        if parts(lo)[0]:
                            act.wait_ge(zc.sem, zc.at(s))
                        nc.scalar.activation(SCR[:, j, :], ring_bank("yd", j)[:, :], ACT.Copy)\
                          .then_inc(yd.sem, 1)
                if (n, at) == (2, 0):
                    rsqrt("o", c)
                if (n, at) == (4, 0):
                    rsqrt("x1", c)
                if (n, at) == (4, 3):
                    for k in range(KM):
                        act.wait_ge(full["x1t"].sem, full["x1t"].at(c, k + 1))
                        act.wait_ge(full["up"].sem, full["up"].at(c - 1))
                        nc.scalar.activation(X1T[:, k, :], ring_bank("x1t", k)[:, :], ACT.Copy)\
                          .then_inc(x1t.sem, 1)
                if (n, at) == (FS + 1, 0):
                    act.wait_ge(rt.sem, rt.at(c, 2))
                    nc.scalar.activation(RP[:, :, :], RP[:, :, :], ACT.Exp).then_inc(rex.sem, 1)
                if (n, at) == (FS + SH, 1):
                    act.wait_ge(full["cf"].sem, full["cf"].at(c))
                    if parts(lo)[0]:
                        act.wait_ge(full["dl"].sem, full["dl"].at(s))
                        act.wait_ge(full["ct"].sem, full["ct"].at(s))
                        act.wait_ge(blo.sem, blo.at(s))
                    nc.scalar.activation(XD[ROW_K:ROW_K + KC, :], ring_bank("cf", 0)[0:KC, :],
                                         ACT.Copy).then_inc(cff.sem, 1)
                    act.wait_ge(cff.sem, cff.at(c))
                    act.wait_ge(full["cb"].sem, full["cb"].at(c - 1))
                    nc.scalar.activation(HL[ROW_K:ROW_K + KC, o, :], XD[ROW_K:ROW_K + KC, :],
                                         ACT.Copy).then_inc(cfh.sem, 1)
                f = n - FS
                if 0 <= f < F and at == 2:
                    act.wait_ge(gate_full.sem, gate_full.at(c, f + 1))
                    act.wait_ge(hf.sem, hf.at(c, up_used(f - 1)))
                    nc.scalar.activation(TG[:, :], GK[:, :], ACT.Tanh).then_inc(tg.sem, 1)
                if 0 <= f < F and at == 3:
                    act.wait_ge(full["up"].sem, full["up"].at(c, f + 1))
                    nc.scalar.activation(UP[:, :], ring_bank("up", f)[:, :], ACT.Copy)\
                      .then_inc(up.sem, 1)
                    if f > SH:
                        coef_take(c, f - SH)

            def prep_part(s, lo, o, n, at):
                c = s + 1

                def x_in(j):
                    act.wait_ge(full["xin"].sem, full["xin"].at(c, j + 1))
                    act.wait_ge(conv.sem, conv.at(c - 1))
                    nc.scalar.activation(XIN[:, j, TAPS - 1:], ring_bank("xin", j)[:, :], ACT.Copy)\
                      .then_inc(xin.sem, 1)

                def z(a):
                    act.wait_ge(full["z"].sem, full["z"].at(c, a + 1))
                    act.wait_ge(sz.sem, sz.at(c, a))
                    nc.scalar.activation(TZ[:, :], ring_bank("z", a)[:, :], ACT.Tanh)\
                      .then_inc(tz.sem, 1)
                    nc.scalar.activation(ZC[:, :], ring_bank("z", a)[:, :], ACT.Copy)\
                      .then_inc(tz.sem, 1)

                def delta(j):
                    act.wait_ge(full["dl"].sem, full["dl"].at(c, j + 1))
                    if j == 0:
                        act.wait_ge(du.sem, du.at(c - 2))
                        act.wait_ge(full["z"].sem, full["z"].at(c))
                        if parts(lo)[1]:
                            act.wait_ge(full["x1t"].sem, full["x1t"].at(s - 1))
                    nc.scalar.activation(ZB[:, j, :], ring_bank("dl", j)[:, :], ACT.Abs,
                                         bias=BDT[:, j:j + 1]).then_inc(absrelu.sem, 1)
                    nc.scalar.activation(DL[:, o, j, :], ring_bank("dl", j)[:, :], ACT.Relu,
                                         bias=BDT[:, j:j + 1]).then_inc(absrelu.sem, 1)

                if (n, at) == (0, 3):
                    rsqrt("xa", c)
                if (n, at) == (2, 2):
                    for k in range(KM):
                        act.wait_ge(full["xt"].sem, full["xt"].at(c, k + 1))
                        act.wait_ge(dadd.sem, dadd.at(c - 1))
                        nc.scalar.activation(XT[:, k, :], ring_bank("xt", k)[:, :], ACT.Copy)\
                          .then_inc(xt.sem, 1)
                if (n, at) == (2, 3):
                    act.wait_ge(conv.sem, conv.at(c - 1))
                    act.wait_ge(halo.sem, halo.at(c - 1))
                    nc.scalar.activation(XIN[:, :, 0:TAPS - 1], HALO[:, o, :, :], ACT.Copy)\
                      .then_inc(halo.sem, 1)
                    x_in(0)
                    x_in(1)
                if n == 3 and 1 <= at < 3:
                    x_in(at + 1)
                if (n, at) == (3, 3):
                    act.wait_ge(xin.sem, xin.at(c))
                    nc.scalar.activation(HALO[:, o, :, :], XIN[:, :, T:], ACT.Copy)\
                      .then_inc(halo.sem, 1)
                    z(0)
                if 4 <= n < 4 + J and at == 0:
                    j = n - 4
                    act.wait_ge(conv.sem, conv.at(c, TAPS * (j + 1)))
                    act.wait_ge(u_s.sem, u_s.at(c, j))
                    nc.scalar.activation(TC[:, :], SCR[:, j, :], ACT.Tanh).then_inc(tc.sem, 1)
                if (n, at) == (4, 1):
                    z(1)
                if n in (6, 7) and at == 3:
                    z(n - 4)
                if (n, at) == (7, 3):
                    act.wait_ge(full["xd"].sem, full["xd"].at(c))
                    if parts(lo)[1]:
                        act.wait_ge(cflo.sem, cflo.at(s - 1))
                    act.wait_ge(full["dl"].sem, full["dl"].at(c - 1))
                    act.wait_ge(full["ct"].sem, full["ct"].at(c - 1))
                    act.wait_ge(blo.sem, blo.at(c - 1))
                    nc.scalar.activation(XD[0:XD_ROWS, :], ring_bank("xd", 0)[0:XD_ROWS, :], ACT.Copy)\
                      .then_inc(xd.sem, 1)
                    act.wait_ge(xd.sem, xd.at(c))
                    act.wait_ge(bk_full.sem, bk_full.at(c - 2))
                    nc.scalar.activation(HL[0:ROW_B2 + NS, o, :], XD[0:ROW_B2 + NS, :], ACT.Copy)\
                      .then_inc(bhi.sem, 1)
                if (n, at) == (8, 3):
                    act.wait_ge(full["ct"].sem, full["ct"].at(c))
                    act.wait_ge(add_c.sem, add_c.at(c - 2))
                    nc.scalar.activation(CT[:, o, :, :].rearrange("p a n -> p (a n)"),
                                         ring_bank("ct", 0)[:, 0:NT * NS], ACT.Copy).then_inc(ct.sem, 1)
                    delta(0)
                    delta(1)
                if (n, at) == (9, 3):
                    delta(2)
                    delta(3)
                if (n, at) == (10, 0):
                    act.wait_ge(absrelu.sem, absrelu.at(c))
                    nc.scalar.activation(ZB[:, :, :], ZB[:, :, :], ACT.Exp, scale=-1.0)\
                      .then_inc(zex.sem, 1)
                    act.wait_ge(zex.sem, zex.at(c))
                    act.wait_ge(u_s.sem, u_s.at(c))
                    nc.scalar.activation(SCR[:, :, :], ZB[:, :, :], ACT.Ln, bias=1.0)\
                      .then_inc(ln.sem, 1)

            run(act, body)

        @block.vector
        def _(dve):
            nc.vector.memset(WX[:, :, :], 0.0)
            nc.vector.memset(HALO[:, :, :, :], 0.0)
            nc.vector.memset(CARRY[:, :, :, :], 0.0)
            nc.vector.memset(COEF[:, :, :], 0.0)
            nc.vector.memset(EPST[:, :], EPS).then_inc(zeroed.sem, 1)
            dve.wait_ge(const_ld.sem, CONST_LOADS)
            dve.wait_ge(ident_made.sem, IDENT_MADE)
            dve.wait_ge(a_exp.sem, 1)
            nc.vector.tensor_scalar(WIN[:, :, DI:2 * DI], WIN[:, :, DI:2 * DI], 0.5, None, ALU.mult)
            nc.vector.tensor_scalar(WG[:, :, :, :], WG[:, :, :, :], 0.5, None, ALU.mult)
            nc.vector.tensor_scalar(CW[:, :, :], CW[:, :, :], 0.5, None, ALU.mult)
            nc.vector.tensor_scalar(CB_[:, :], CB_[:, :], 0.5, None, ALU.mult)
            nc.vector.tensor_scalar(ANEG[:, :, :], ANEG[:, :, :], -1.0, None, ALU.mult)
            nc.vector.tensor_copy(SEL[:, :], SELF)
            for j in range(J):
                last = nc.vector.tensor_scalar(DIAG[:, j, :], IDN[:, :], DSK[:, j:j + 1], None, ALU.mult)
            last.then_inc(consts.sem, 1)
            dve.wait_ge(consts.sem, 1)

            def scan_step(s, r, n, j):
                dve.wait_ge(ex.sem, ex.at(s, n * J + j + 1))
                if j % 2 == 0:
                    dve.wait_ge(bu.sem, bu.at(s, 2 * n + j // 2 + 1))
                if j == 0:
                    if n < 2:
                        dve.wait_ge(ht_full.sem, ht_full.at(s - 1, NT * (NS + n)))
                    else:
                        dve.wait_ge(ht_full.sem, ht_full.at(s, NT * n))
                    dve.wait_ge(carry.sem, carry.at(s, n))
                nc.vector.tensor_tensor_scan(H[:, n % 2, j, :], DA[:, j, :],
                                             BU[:, (2 * n + j // 2) % 4, j % 2, :],
                                             CARRY[:, r, n, j:j + 1], ALU.mult, ALU.add)\
                  .then_inc(scan.sem, 1)

            def add_state(s, r, n, a):
                dve.wait_ge(ht_full.sem, ht_full.at(s, NT * (n + 1) + a + 1))
                if n == 0:
                    dve.wait_ge(yinit.sem, yinit.at(s, a + 1))
                    dve.wait_ge(ct.sem, ct.at(s))
                else:
                    dve.wait_ge(add_c.sem, add_c.at(s, (n - 1) * NT + a + 1))
                nc.vector.scalar_tensor_tensor(YT[:, a, :], HT[(NT * (n + 1) + a) % 2][:, :],
                                               CT[:, r, a, n:n + 1], YT[:, a, :],
                                               ALU.mult, ALU.add).then_inc(add_c.sem, 1)

            def moments(w, c, a, tile):
                nc.vector.bn_stats(ST[w][:, a, :], tile).then_inc(stats[w].sem, 1)

            def moments_end(w, c):
                dve.wait_ge(stats[w].sem, stats[w].at(c, NT))
                dve.wait_ge(rstd[w].sem, rstd[w].at(c - 1))
                dve.sem_inc(waited, 1)
                for a in range(NT):
                    nc.vector.bn_aggr(MV[w][:, a, :], ST[w][:, a, :]).then_inc(stats[w].sem, 1)

            def normed(w, c, a, dst, src):
                dve.wait_ge(rstd[w].sem, rstd[w].at(c))
                nc.vector.tensor_scalar(dst, src, MV[w][:, a, 0:1], RS[w][:, a:a + 1],
                                        ALU.subtract, ALU.mult).then_inc(norm[w].sem, 1)

            def dn(a):
                return DN[a // 2][:, (a % 2) * DM:(a % 2 + 1) * DM]

            def body(s, lo, r):
                with_scan, ffn, prep = parts(lo)
                o = 1 - r
                for n in range(NS):
                    for j in range(J):
                        if with_scan:
                            scan_step(s, r, n, j)
                        if ffn:
                            ffn_part(s, lo, o, n, 2 * j)
                        if prep:
                            prep_part(s, lo, o, n, 2 * j)
                        if with_scan and n > 0:
                            add_state(s, r, n - 1, j)
                        if ffn:
                            ffn_part(s, lo, o, n, 2 * j + 1)
                        if prep:
                            prep_part(s, lo, o, n, 2 * j + 1)
                    if with_scan:
                        dve.wait_ge(scan.sem, scan.at(s, (n + 1) * J))
                        nc.vector.tensor_copy(CARRY[:, r, n, :], H[:, n % 2, :, T - 1])\
                          .then_inc(carry.sem, 1)
                    if ffn:
                        ffn_end(s, lo, n)
                if ffn:
                    for a in range(NT):
                        dve.wait_ge(down.sem, down.at(s - 1))
                        moments("y", s - 1, a, dn(a))
                    moments_end("y", s - 1)
                if with_scan:
                    for a in range(NT):
                        add_state(s, r, NS - 1, a)
                if with_scan:
                    for a in range(NT):
                        dve.wait_ge(add_c.sem, add_c.at(s, (NS - 1) * NT + a + 1))
                        nc.vector.tensor_tensor(YT[:, a, :], YT[:, a, :], SZ[:, r, a, :], ALU.mult)\
                          .then_inc(y_gate.sem, 1)
                if ffn:
                    for a in range(NT):
                        if prep and a == 0:
                            dve.wait_ge(dadd.sem, dadd.at(s + 1))
                        normed("y", s - 1, a, XN[:, a, :], dn(a))
                    dve.wait_ge(norm["y"].sem, norm["y"].at(s - 1))
                    nc.vector.tensor_tensor(XR[:, :, :], XR[:, :, :], XN, ALU.add)\
                      .then_inc(y_add.sem, 1)

            def over(t):
                return t.unsqueeze(2).to_broadcast([P, NT, E])

            def route(c, i):
                if i == 2:
                    dve.wait_ge(rex.sem, rex.at(c))
                elif i > 0:
                    dve.wait_ge(rt.sem, rt.at(c, i))
                logits = DN[0][:, 0:NT * E].rearrange("p (a e) -> p a e", a=NT)
                if i == 0:
                    dve.wait_ge(rt_full.sem, rt_full.at(c))
                    last = nc.vector.tensor_reduce(RMAX, logits, X, ALU.max)
                elif i == 1:
                    last = nc.vector.tensor_tensor(RP[:, :, :], logits, over(RMAX), ALU.subtract)
                elif i == 2:
                    last = nc.vector.tensor_reduce(RSUM, RP[:, :, :], X, ALU.add)
                elif i == 3:
                    last = nc.vector.reciprocal(RINV, RSUM)
                elif i == 4:
                    last = nc.vector.tensor_tensor(RP[:, :, :], RP[:, :, :], over(RINV), ALU.mult)
                elif i in (5, 11):
                    src = RP if i == 5 else RL
                    last = nc.vector.tensor_reduce(R1, src[:, :, :], X, ALU.max)
                elif i in (6, 12):
                    src = RP if i == 6 else RL
                    last = nc.vector.tensor_tensor(RQ[:, :, :], src[:, :, :], over(R1), ALU.is_equal)
                elif i in (7, 13):
                    last = nc.vector.tensor_tensor(RQ[:, :, :], RQ[:, :, :], RANKS[:, :].unsqueeze(1).to_broadcast([P, NT, E]), ALU.mult)
                elif i in (8, 14):
                    last = nc.vector.tensor_reduce(R1, RQ[:, :, :], X, ALU.max)
                elif i in (9, 15):
                    dst = RM if i == 9 else RQ
                    last = nc.vector.tensor_tensor(dst[:, :, :], RQ[:, :, :], over(R1), ALU.is_equal)
                elif i == 10:
                    last = nc.vector.scalar_tensor_tensor(RL[:, :, :], RM[:, :, :], -4.0, RP[:, :, :],
                                                          ALU.mult, ALU.add)
                elif i == 16:
                    last = nc.vector.tensor_tensor(RM[:, :, :], RM[:, :, :], RQ[:, :, :], ALU.add)
                else:
                    at = 0 if i == 17 else ROW_K2 - ROW_K
                    last = nc.vector.tensor_tensor(COEF[:, :, at:at + E], RM[:, :, :], RP[:, :, :],
                                                   ALU.mult)
                last.then_inc(rt.sem, 1)

            def ffn_part(s, lo, o, n, pos):
                c = s - 1
                if n == 1 and pos in (1, 2, 6, 7):
                    a = (1, 2, 6, 7).index(pos)
                    dve.wait_ge(o_full.sem, o_full.at(c, 2 * (a // 2) + 2))
                    moments("o", c, a, dn(a))
                if n == 2 and pos >= 8 - NT:
                    a = pos - (8 - NT)
                    if a == 0 and parts(lo)[0]:
                        dve.wait_ge(dadd.sem, dadd.at(s))
                    normed("o", c, a, XN[:, a, :], dn(a))
                if n == 3 and pos >= 8 - NT:
                    a = pos - (8 - NT)
                    dve.wait_ge(x1_add.sem, x1_add.at(c, a // 2 + 1))
                    moments("x1", c, a, XR[:, a, :])
                if n == 4 and pos >= 8 - NT:
                    a = pos - (8 - NT)
                    normed("x1", c, a, XN[:, a, :], XR[:, a, :])
                if n == FS + 1 and pos >= 3:
                    first = 2 + 4 * (pos - 3)
                    for i in range(first, min(first + 4, RT_STEPS)):
                        route(c, i)
                f = n - FS - 1
                if 0 <= f < F and pos == 1:
                    dve.wait_ge(tg.sem, tg.at(c, f + 1))
                    nc.vector.scalar_tensor_tensor(TG[:, :], TG[:, :], 1.0, GK[:, :],
                                                   ALU.add, ALU.mult).then_inc(hid.sem, 1)

            def ffn_end(s, lo, n):
                c = s - 1
                if n == 1:
                    moments_end("o", c)
                if n == 3:
                    moments_end("x1", c)
                if n == FS:
                    route(c, 0)
                    route(c, 1)
                if n == FS + SH:
                    dve.wait_ge(cfh.sem, cfh.at(c))
                    rows = slice(ROW_K2, ROW_K2 + E)
                    nc.vector.tensor_tensor(HL[rows, 1 - lo % 2, :], XD[rows, :],
                                            HL[rows, 1 - lo % 2, :].bitcast(f32), ALU.subtract)\
                      .then_inc(cflo.sem, 1)

            def prep_part(s, lo, o, n, pos):
                c = s + 1
                if n == 0 and pos < NT:
                    dve.wait_ge(xa_ld.sem, xa_ld.at(c))
                    moments("xa", c, pos, XA[:, pos, :])
                if n == 0 and pos == NT:
                    moments_end("xa", c)
                if n == 1 and 3 <= pos < 3 + NT:
                    normed("xa", c, pos - 3, XA[:, pos - 3, :], XA[:, pos - 3, :])
                if (n, pos) in ((4, 0), (5, 0), (7, 2), (8, 2)):
                    a = (4, 5, 7, 8).index(n)
                    dve.wait_ge(tz.sem, tz.at(c, 2 * (a + 1)))
                    nc.vector.scalar_tensor_tensor(SZ[:, o, a, :], TZ[:, :], 1.0, ZC[:, :],
                                                   ALU.add, ALU.mult).then_inc(sz.sem, 1)
                step = 8 * (n - 3) + pos - 3
                if step >= 0 and step % 2 == 0 and step // 8 < J:
                    j, k = step // 8, step % 8 // 2
                    if k == 0:
                        dve.wait_ge(xin.sem, xin.at(c, j + 1))
                        if j == 0:
                            dve.wait_ge(halo.sem, halo.at(c, 1))
                            dve.wait_ge(zc.sem, zc.at(c - 1))
                            if parts(lo)[1]:
                                dve.wait_ge(o_full.sem, o_full.at(s - 1))
                        nc.vector.tensor_scalar(SCR[:, j, :], XIN[:, j, 0:T], CW[:, j, 0:1],
                                                CB_[:, j:j + 1], ALU.mult, ALU.add)\
                          .then_inc(conv.sem, 1)
                    else:
                        dve.wait_ge(conv.sem, conv.at(c, TAPS * j + k))
                        nc.vector.scalar_tensor_tensor(SCR[:, j, :], XIN[:, j, k:k + T],
                                                       CW[:, j, k:k + 1], SCR[:, j, :],
                                                       ALU.mult, ALU.add).then_inc(conv.sem, 1)
                if 4 <= n < 4 + J and pos == 6:
                    j = n - 4
                    dve.wait_ge(tc.sem, tc.at(c, j + 1))
                    if j == 0:
                        dve.wait_ge(ht_full.sem, ht_full.at(s, NT))
                        dve.wait_ge(du.sem, du.at(s))
                    nc.vector.scalar_tensor_tensor(U[:, j, :], TC[:, :], 1.0, SCR[:, j, :],
                                                   ALU.add, ALU.mult).then_inc(u_s.sem, 1)
                if (n, pos) == (8, 4):
                    dve.wait_ge(bhi.sem, bhi.at(c))
                    rows = slice(ROW_B2, ROW_B2 + NS)
                    nc.vector.tensor_tensor(HL[rows, o, :], XD[rows, :],
                                            HL[rows, o, :].bitcast(f32), ALU.subtract)\
                      .then_inc(blo.sem, 1)
                if n in (11, 12) and pos % 2 == 0:
                    j = 2 * (n - 11) + pos // 4
                    if pos % 4 == 0:
                        dve.wait_ge(ln.sem, ln.at(c))
                        nc.vector.tensor_tensor(DL[:, o, j, :], DL[:, o, j, :], SCR[:, j, :], ALU.add)\
                          .then_inc(lsum.sem, 1)
                    else:
                        dve.wait_ge(lsum.sem, lsum.at(c, j + 1))
                        nc.vector.tensor_scalar(SCR[:, j, :], ZB[:, j, :], 1.0, -1.0,
                                                ALU.add, ALU.add).then_inc(w1.sem, 1)

            run(dve, body)

        @block.gpsimd
        def _(pool):
            nc.gpsimd.memset(IDN[:, :], 0.0).then_inc(ident_made.sem, 1)
            nc.gpsimd.memset(SELF, 0.0).then_inc(ident_made.sem, 1)
            pool.wait_ge(ident_made.sem, 2)
            nc.gpsimd.affine_select(out=IDN[:, :], in_=IDN[:, :], compare_op=ALU.not_equal, fill=1.0,
                                    base=0, pattern=[[-1, P]], channel_multiplier=1)\
              .then_inc(ident_made.sem, 1)
            for q in range(P // 32):
                pool.wait_ge(ident_made.sem, 3 + q)
                nc.gpsimd.affine_select(out=SELF, in_=SELF, compare_op=ALU.not_equal,
                                        fill=1.0, base=-32 * q, pattern=[[-1, NS]],
                                        channel_multiplier=1).then_inc(ident_made.sem, 1)
            for e in range(E):
                nc.gpsimd.memset(RANKS[:, e:e + 1], float(E - e)).then_inc(ident_made.sem, 1)

            def inflow(s, n, h):
                pool.wait_ge(bb.sem, bb.at(s, n + 1))
                if n == 0:
                    pool.wait_ge(du.sem, du.at(s, 2 * h + 2))
                if n < 2:
                    pool.wait_ge(scan.sem, scan.at(s - 1, (n + NS - 2) * J + 2 * h + 2))
                else:
                    pool.wait_ge(scan.sem, scan.at(s, (n - 2) * J + 2 * h + 2))
                nc.gpsimd.tensor_tensor(BU[:, (2 * n + h) % 4, :, :], DU[:, 2 * h:2 * h + 2, :],
                                        BB[:, n % 2, :].unsqueeze(1).to_broadcast([P, 2, T]),
                                        ALU.mult).then_inc(bu.sem, 1)

            def body(s, lo, r):
                with_scan, ffn, prep = parts(lo)
                o = 1 - r
                if with_scan:
                    inflow(s, 0, 0)
                    inflow(s, 0, 1)
                for n in range(NS):
                    if with_scan and n + 1 < NS:
                        inflow(s, n + 1, 0)
                    f = n - FS - 1
                    if ffn and 0 <= f < F:
                        hidden(s - 1, f)
                    if with_scan and n + 1 < NS:
                        inflow(s, n + 1, 1)
                    if ffn and n == 2:
                        pool.wait_ge(xr_ld.sem, xr_ld.at(s - 1))
                        for h in range(2):
                            pool.wait_ge(norm["o"].sem, norm["o"].at(s - 1, 2 * h + 2))
                            tiles = slice(2 * h, 2 * h + 2)
                            nc.gpsimd.tensor_tensor(XR[:, tiles, :], XR[:, tiles, :], XN[:, tiles, :],
                                                    ALU.add).then_inc(x1_add.sem, 1)
                    if prep:
                        prep_part(s + 1, s, o, n)

            def hidden(c, f):
                pool.wait_ge(hid.sem, hid.at(c, f + 1))
                pool.wait_ge(up.sem, up.at(c, f + 1))
                pool.wait_ge(down.sem, down.at(c, f))
                nc.gpsimd.tensor_tensor(HF[:, :], TG[:, :], UP[:, :], ALU.mult).then_inc(hf.sem, 1)
                if f >= SH:
                    pool.wait_ge(hf.sem, hf.at(c, hf_done(f) - 1))
                    pool.wait_ge(cb.sem, cb.at(c, f - SH + 1))
                    nc.gpsimd.tensor_tensor(HF[:, :], HF[:, :], CB[:, :], ALU.mult)\
                      .then_inc(hf.sem, 1)

            def prep_part(c, s, o, n):
                for j in {11: (0,), 12: (1, 2), 13: (3,)}.get(n, ()):
                    pool.wait_ge(w1.sem, w1.at(c, j + 1))
                    nc.gpsimd.tensor_tensor(ZB[:, j, :], ZB[:, j, :], SCR[:, j, :], ALU.subtract)\
                      .then_inc(zc.sem, 1)
                for j in {13: (0,), 14: (1, 2), 15: (3,)}.get(n, ()):
                    pool.wait_ge(zc.sem, zc.at(c, j + 1))
                    pool.wait_ge(lsum.sem, lsum.at(c, j + 1))
                    nc.gpsimd.tensor_tensor(DL[:, o, j, :], DL[:, o, j, :], ZB[:, j, :], ALU.add)\
                      .then_inc(dadd.sem, 1)
                if n == 15:
                    for j in range(J):
                        pool.wait_ge(dadd.sem, dadd.at(c, j + 1))
                        pool.wait_ge(u_s.sem, u_s.at(c))
                        if j == 0:
                            pool.wait_ge(bu.sem, bu.at(s))
                        nc.gpsimd.tensor_tensor(DU[:, j, :], DL[:, o, j, :], U[:, j, :], ALU.mult)\
                          .then_inc(du.sem, 1)

            run(pool, body)


_INS = ["L0_attn_x", "L0_attn_W_in", "L0_attn_conv_w", "L0_attn_conv_b", "L0_attn_W_xproj",
        "L0_attn_W_dt", "L0_attn_b_dt", "L0_attn_A_log", "L0_attn_D_skip", "L0_attn_W_out",
        "L0_ffn_router", "L0_ffn_experts_gate", "L0_ffn_experts_up", "L0_ffn_experts_down",
        "L0_ffn_shared_gate", "L0_ffn_shared_up", "L0_ffn_shared_down"]


def kernel(**inputs):
    import numpy as _np
    import concourse.bacc as _bacc
    from concourse import mybir as _mybir
    from concourse.bass_utils import run_bass_kernel_spmd as _run

    nc = _bacc.Bacc("TRN2", target_bir_lowering=False, num_devices=1)
    arrays, args = {}, []
    for name in _INS:
        a = _np.ascontiguousarray(inputs[name])
        arrays[name + "_in"] = a
        args.append(nc.dram_tensor(name + "_in", a.shape, _mybir.dt.from_np(a.dtype),
                                   kind="ExternalInput").ap())
    shape = inputs["L0_attn_x"].shape
    args.append(nc.dram_tensor("out", shape, _mybir.dt.float32, kind="ExternalOutput").ap())
    mamba_moe_kernel(nc, *args)
    r = _run(nc, [arrays], core_ids=[0])
    return r.results[0]["out"]
```

```python
from contextlib import ExitStack

import concourse.bass as bass
from concourse import mybir


class Stage:

    def __init__(self, sem, per):
        self.sem, self.per = sem, per

    def at(self, chunk, k=None):
        value = chunk * self.per + (self.per if k is None else k)
        return max(value, 0) if isinstance(value, int) else value


def mamba_moe_kernel(nc, x, w_in, conv_w, conv_b, w_xproj, w_dt, b_dt, a_log, d_skip, w_out,
                     router, e_gate, e_up, e_down, s_gate, s_up, s_down, out):
    f32 = mybir.dt.float32
    ALU, ACT, X = mybir.AluOpType, mybir.ActivationFunctionType, mybir.AxisListType.X
    P = 128
    BATCH, LENGTH, DM = x.shape
    DI, TAPS = conv_w.shape[0], conv_w.shape[2]
    NS = a_log.shape[1]
    RANK = w_dt.shape[0]
    E = router.shape[1]
    T = 512
    NT = T // P
    KM = DM // P
    J = DI // P
    SH = s_gate.shape[1] // P
    F = SH + E
    CHUNKS = BATCH * LENGTH // T
    EPS = 1e-5
    ROW_B, ROW_DT, ROW_C, ROW_K = 0, 32, 64, 96
    XD_ROWS = ROW_C + NS
    HTS = 3

    with ExitStack() as ctx:
        def sb(name, shape, dt=f32):
            return ctx.enter_context(nc.sbuf_tensor(name, shape, dt))

        def ps(name):
            return ctx.enter_context(nc.psum_tensor(name, [P, 512], f32))

        def stage(name, per):
            return Stage(ctx.enter_context(nc.semaphore(name)), per)

        WIN = sb("w_in_sb", [P, KM, 2 * DI])
        WG = sb("w_gate_sb", [P, KM, F, P])
        WU = sb("w_up_sb", [P, KM, F, P])
        WD = sb("w_down_sb", [P, F, DM])
        WO = sb("w_out_sb", [P, J, DM])
        WX = sb("w_xproj_sb", [P, J, XD_ROWS])
        WDT = sb("w_dt_sb", [P, DI])
        WR = sb("router_sb", [P, KM, E])
        CW = sb("conv_w_sb", [P, J, TAPS])
        CB_ = sb("conv_b_sb", [P, J])
        BDT = sb("b_dt_sb", [P, J])
        DSK = sb("d_skip_sb", [P, J])
        ANEG = sb("a_neg", [P, J, NS])
        EPST, ONE = sb("eps", [P, 1]), sb("one", [P, 1])
        IDN = sb("ident", [P, P])
        DIAG = sb("diag_d", [P, J, P])
        RANKS = sb("ranks", [P, E])
        XA = sb("xa", [P, NT, DM])
        ZB = sb("z_buf", [P, J, T])
        XN = ZB[:, 0:2, :].rearrange("p j t -> p (j t)").rearrange("p (a d) -> p a d", a=NT)
        XT = ZB[:, 2:4, :]
        SCR = sb("scratch", [P, J, T])
        XIN = sb("xin", [P, J, T + TAPS - 1])
        HALO = sb("halo", [P, BATCH, J, TAPS - 1])
        U = sb("u", [P, J, T])
        TC = sb("tanh_conv", [P, T])
        TZ = sb("tanh_z", [P, T])
        ZC = sb("z_copy", [P, T])
        SZ = sb("silu_z", [P, 2, NT, DI])
        DL = sb("delta", [P, 2, J, T])
        DU = sb("delta_u", [P, J, T])
        XD = sb("x_dbl", [P, 2, T])
        CT = sb("c_t", [P, 2, NT, NS])
        BB = sb("b_rows", [P, 2, T])
        DA = sb("d_a", [P, J, T])
        BU = sb("d_bu", [P, 4, 2, T])
        H = sb("h", [P, 2, J, T])
        CARRY = sb("carry", [P, BATCH, NS, J])
        YT = sb("y_t", [P, NT, DI])
        XR = sb("xr", [P, NT, DM])
        X1T = sb("x1_t", [P, KM, T])
        TG = sb("tanh_gate", [P, T])
        HF = sb("hidden", [P, T])
        UP = sb("up", [P, T])
        CB = sb("coef_rows", [P, 2, T])
        ST = {w: sb(f"stats_{w}", [P, NT, 6]) for w in ("xa", "o")}
        ST["x1"] = ST["y"] = ST["o"]
        MV = {w: sb(f"mean_var_{w}", [P, NT, 2]) for w in ("xa", "o", "x1", "y")}
        RS = {w: sb(f"rstd_{w}", [P, NT]) for w in ("xa", "o", "x1", "y")}
        MR = {w: sb(f"mean_rstd_{w}", [P, NT]) for w in ("xa", "o", "y")}
        R_SMALL = sb("r_small", [P, 4, NT])
        RMAX, RSUM, RINV, R1 = (R_SMALL[:, i, :] for i in range(4))
        RP = sb("r_prob", [P, NT, E])
        RQ = sb("r_equal", [P, NT, E])
        RM = sb("r_mask", [P, NT, E])
        RL = sb("r_left", [P, NT, E])
        COEF = sb("coef", [P, NT, E])

        HT = [ps(f"ht{i}") for i in range(HTS)]
        DN = [ps("dn0"), ps("dn1")]
        GK = ps("gate_bank")
        RING = [ps("ring0"), ps("ring1")]

        const_ld, xa_ld = stage("const_ld", 0), stage("xa_ld", 16)
        xr_ld, out_st = stage("xr_ld", 16), stage("out_st", 16)
        bb_ld = [stage(f"bb{i}_ld", 16 * NS // 2) for i in range(2)]
        cb_ld = [stage(f"cb{i}_ld", 16 * E // 2) for i in range(2)]
        zeroed, ident_made, consts = stage("zeroed", 0), stage("ident_made", 0), stage("consts", 0)
        a_exp, ffn_ld, ffn_consts = stage("a_exp", 0), stage("ffn_ld", 0), stage("ffn_consts", 0)
        ht_full = stage("ht_full", NT * (NS + 1))
        full = {w: stage(f"{w}_full", n) for w, n in dict(
            yd=J, xt=KM, xin=J, z=NT, x1t=KM, up=F, cf=1, xd=1, ct=1, dl=J).items()}
        o_full, rt_full = stage("o_full", NT), stage("rt_full", 1)
        gate_full, down = stage("gate_full", F), stage("down", F)
        ex = stage("ex", NS * J)
        yd, yinit, xt = stage("yd", J), stage("yinit", NT), stage("xt", KM)
        rstd = {w: stage(f"rstd_{w}_s", 2) for w in ("xa", "o", "x1", "y")}
        halo, xin, tz = stage("halo_s", 2), stage("xin_s", J), stage("tz_s", 3 * NT)
        x1t, tc, tg, up = stage("x1t_s", KM), stage("tc_s", 2 * J), stage("tg_s", F), stage("up_s", F)
        rex, cff = stage("rex", 1), stage("cff", 1)
        xd, ct = stage("xd_s", 1), stage("ct_s", 1)
        absrelu, zex = stage("absrelu", 2 * J), stage("zex", 2)
        wexp, ln, tap0 = stage("wexp", 2), stage("ln", 1), stage("tap0", J)
        shift = {w: stage(f"shift_{w}", NT if w == "o" else NT + 1) for w in ("xa", "o", "y")}
        stream = {w: stage(f"stream_{w}", NT) for w in ("o", "y")}
        scan, add_c, carry = stage("scan", NS * J), stage("add_c", NS * NT), stage("carry_s", NS)
        stats = {w: stage(f"stats_{w}_s", 2 * NT) for w in ("xa", "o", "x1", "y")}
        norm = {w: stage(f"norm_{w}", NT) for w in ("xa", "x1")}
        resid = {w: stage(f"resid_{w}", NT) for w in ("o", "y")}
        y_gate = stage("y_gate", NT)
        conv, u_s, sz = stage("conv", J * (TAPS - 1)), stage("u_s", J), stage("sz", NT)
        RT_STEPS = 18
        rt = stage("rt", RT_STEPS)
        hid = stage("hid", F)
        corr, lsum, dadd_v = stage("corr", J), stage("lsum", J), stage("dadd_v", 1)
        waited = ctx.enter_context(nc.semaphore("waited"))
        bu = stage("bu", 2 * NS)
        hf = stage("hf", SH + 2 * E)
        dadd, du = stage("dadd", J - 1), stage("du", J)

        def hf_done(k):
            return k + 1 if k < SH else SH + 2 * (k + 1 - SH)

        def up_used(k):
            return k + 1 if k < SH else hf_done(k) - 1

        FS = 5
        RING_USE = [("yd", -1, j) for j in range(J)]
        RING_USE += [("z", 1, 0), ("z", 1, 1), ("xin", 1, 2), ("z", 1, 2), ("xin", 1, 3)]
        RING_USE += [("x1t", -1, k) for k in range(KM)]
        RING_USE += [("up", -1, 0), ("up", -1, 1), ("z", 1, 3)]
        RING_USE += [("up", -1, 2), ("cf", -1, 0), ("xd", 1, 0)]
        RING_USE += [("up", -1, 3), ("dl", 1, 0), ("dl", 1, 1), ("dl", 1, 2), ("dl", 1, 3)]
        RING_USE += [("up", -1, k) for k in range(4, F - 1)] + [("ct", 1, 0)]
        RING_USE += [("xt", 2, k) for k in range(KM)] + [("up", -1, F - 1), ("xin", 2, 0), ("xin", 2, 1)]
        TANH_CONV = ((3, 0), (4, 3), (5, 3), (6, 3))
        TAP = (((2, 2), (2, 4), (2, 6)), ((3, 7), (4, 1), (4, 3)),
               ((5, 1), (5, 3), (5, 5)), ((6, 1), (6, 3), (6, 5)))
        LSUM_AT = ((12, 2), (12, 6), (13, 6), (14, 6))
        SZ_POOL = (2, 3, 4, 7)
        Z_PE, Z_ACT = ((1, 3), (2, 1), (3, 2), (6, 3)), ((2, 0), (3, 0), (3, 3), (7, 1))
        ring_free = {"yd": (yd, 1), "xt": (xt, 1), "xin": (xin, 1), "z": (tz, 3), "x1t": (x1t, 1),
                     "up": (up, 1), "cf": (cff, 1), "xd": (xd, 1), "ct": (ct, 1),
                     "dl": (absrelu, 2)}

        def ring_bank(what, k):
            at = next(i for i, use in enumerate(RING_USE) if use[0] == what and use[2] == k)
            return RING[at % 2]

        def ring_user_before(s, lo, what, k):
            at = next(i for i, use in enumerate(RING_USE) if use[0] == what and use[2] == k)
            back, parity = 0, at % 2
            while lo - back >= -2:
                at -= 1
                if at < 0:
                    at, back = len(RING_USE) - 1, back + 1
                before, part, kb = RING_USE[at]
                if at % 2 == parity and 0 <= lo - back + part < CHUNKS:
                    freed, per = ring_free[before]
                    return freed.sem, freed.at(s - back + part, per * (kb + 1))
            return yd.sem, 0

        bodies_before = [-2, -1, 0, 1]
        loop_first, loop_last = 2, CHUNKS - 3
        bodies_after = [CHUNKS - 2, CHUNKS - 1, CHUNKS, CHUNKS + 1]

        def run(engine, body):
            for s in bodies_before:
                body(s, s, s % 2)
            with engine.Fori(0, (loop_last - loop_first + 1) // 2) as i:
                for r in range(2):
                    body(2 * i + loop_first + r, loop_first + r, r)
            for s in bodies_after:
                body(s, s, s % 2)

        def parts(lo):
            return exists(lo), exists(lo - 1), exists(lo + 1)

        def exists(chunk):
            return 0 <= chunk < CHUNKS

        def tokens(dram, batch, index):
            return dram[batch, bass.ds(index * T, T), :].rearrange("(a p) d -> p a d", p=P)

        block = ctx.enter_context(nc.Block())

        @block.sync
        def _(sp):
            loads = [
                (WIN[:, :, :], w_in.rearrange("(k p) c -> p k c", p=P)),
                (CW[:, :, :], conv_w.rearrange("(j p) o k -> p j (o k)", p=P)),
                (CB_[:, :], conv_b.rearrange("(j p) -> p j", p=P)),
                (BDT[:, :], b_dt.rearrange("(j p) -> p j", p=P)),
                (DSK[:, :], d_skip.rearrange("(j p) -> p j", p=P)),
                (ANEG[:, :, :], a_log.rearrange("(j p) n -> p j n", p=P)),
                (WDT[ROW_DT:ROW_DT + RANK, :], w_dt),
            ]
            ffn_loads = [
                (WO[:, :, :], w_out.rearrange("(j p) c -> p j c", p=P)),
                (WR[:, :, :], router.rearrange("(k p) e -> p k e", p=P)),
            ]
            for k in range(KM):
                rows = slice(k * P, (k + 1) * P)
                for dst, shared, experts in ((WG, s_gate, e_gate), (WU, s_up, e_up)):
                    ffn_loads.append((dst[:, k, 0:SH, :], shared[rows, :].rearrange("p (g f) -> p g f", g=SH)))
                    ffn_loads.append((dst[:, k, SH:F, :], experts[:, rows, :].rearrange("e p f -> p e f")))
            ffn_loads.append((WD[:, 0:SH, :], s_down.rearrange("(g p) c -> p g c", p=P)))
            ffn_loads.append((WD[:, SH:F, :], e_down.rearrange("e p c -> p e c")))
            sp.dma_start(XA[:, :, :], tokens(x, 0, 0)).then_inc(xa_ld.sem, 16)
            with nc.allow_non_contiguous_dma(reason="512 values each"):
                for dst, src in loads:
                    sp.dma_start(dst, src).then_inc(const_ld.sem, 16)
            sp.wait_ge(zeroed.sem, 1)
            wx = w_xproj.rearrange("(j p) c -> p j c", p=P)
            for row, col in ((ROW_B, RANK), (ROW_DT, 0), (ROW_C, RANK + NS)):
                width = RANK if row == ROW_DT else NS
                sp.dma_start(WX[:, :, row:row + width], wx[:, :, col:col + width])\
                  .then_inc(const_ld.sem, 16)
            with nc.allow_non_contiguous_dma(reason="a router row has 8 values"):
                for dst, src in ffn_loads:
                    sp.dma_start(dst, src).then_inc(ffn_ld.sem, 16)

            def b_row(c, r, n):
                if n < 2:
                    sp.wait_ge(bu.sem, bu.at(c - 1, 2 * (n + NS - 2) + 2))
                else:
                    sp.wait_ge(bu.sem, bu.at(c, 2 * (n - 2) + 2))
                sp.dma_start(BB[:, n % 2, :], over_partitions(XD[ROW_B + n:ROW_B + n + 1, r, :]))\
                  .then_inc(bb_ld[n % 2].sem, 16)

            def coef_row(c, rc, e, prep):
                if e == 0:
                    sp.wait_ge(cff.sem, cff.at(c))
                if e == 1 and prep:
                    sp.wait_ge(xd.sem, xd.at(c + 2))
                if e >= 2:
                    sp.wait_ge(hf.sem, hf.at(c, hf_done(SH + e - 2)))
                sp.dma_start(CB[:, e % 2, :], over_partitions(XD[ROW_K + e:ROW_K + e + 1, rc, :]))\
                  .then_inc(cb_ld[e % 2].sem, 16)

            def over_partitions(row):
                return row.unsqueeze(1).to_broadcast([1, P, T])

            def body(s, lo, r, half):
                with_scan, ffn, prep = parts(lo)
                for n in range(NS):
                    if exists(lo - 2) and n == 1:
                        result, added = tokens(out, r, half - 1), stream["y"].at(s - 2)
                        sp.wait_ge(stream["y"].sem, added)
                        sp.dma_start(result, XR[:, :, :]).then_inc(out_st.sem, 16)
                    if with_scan and n + 2 < NS:
                        b_row(s, r, n + 2)
                    if prep and n + 2 >= NS:
                        if n + 2 == NS and not ffn:
                            sp.wait_ge(xd.sem, xd.at(s + 1))
                        b_row(s + 1, 1 - r, n + 2 - NS)
                    if ffn and n == 1:
                        again, stored = tokens(x, 1 - r, half + r - 1), out_st.at(s - 2)
                        sp.wait_ge(out_st.sem, stored)
                        sp.dma_start(XR[:, :, :], again)\
                          .then_inc(xr_ld.sem, 16)
                    if lo + 2 > 0 and exists(lo + 2) and n == 2:
                        following, transposed = tokens(x, r, half + 1), full["xt"].at(s + 1)
                        sp.wait_ge(full["xt"].sem, transposed)
                        sp.dma_start(XA[:, :, :], following).then_inc(xa_ld.sem, 16)
                    e = n - FS - SH
                    if ffn and 0 <= e < E:
                        coef_row(s - 1, 1 - r, e, prep)

            for s in bodies_before:
                body(s, s, s % 2, s // 2)
            with sp.Fori(0, (loop_last - loop_first + 1) // 2) as i:
                for r in range(2):
                    body(2 * i + loop_first + r, loop_first + r, r, i + loop_first // 2)
            for s in bodies_after:
                body(s, s, s % 2, s // 2)
            sp.wait_ge(out_st.sem, out_st.at(CHUNKS - 1))

        IDENT_MADE = 2 + E
        CONST_LOADS, FFN_LOADS = (7 + 3) * 16, (2 + 4 * KM + 2) * 16

        @block.tensor
        def _(pe):
            pe.wait_ge(consts.sem, 1)
            pe.wait_ge(const_ld.sem, CONST_LOADS)
            pe.wait_ge(ident_made.sem, IDENT_MADE)

            def ht_user_before(s, q):
                if q < HTS:
                    last = max(t for t in range(NT * (NS + 1)) if t % HTS == q)
                    return add_c.sem, add_c.at(s - 1, last - NT + 1)
                if q < NT + HTS:
                    return yinit.sem, yinit.at(s, q - HTS + 1)
                return add_c.sem, add_c.at(s, q - HTS - NT + 1)

            def body(s, lo, r):
                with_scan, ffn, prep = parts(lo)
                if lo == 1:
                    pe.wait_ge(ffn_ld.sem, FFN_LOADS)
                    pe.wait_ge(ffn_consts.sem, 1)
                o = 1 - r
                if with_scan:
                    for a in range(HTS):
                        transpose_du(s, a)
                if ffn:
                    transpose_y(s, lo)
                if with_scan:
                    for a in range(HTS, NT):
                        transpose_du(s, a)
                for n in range(NS):
                    for at in range(1, NT):
                        if with_scan and n > 0:
                            for a in (range(HTS) if at == 1 else (NT - 1,) if at == 2 else ()):
                                transpose_state(s, n - 1, a)
                        if ffn and at == 1 and 0 <= n - FS - 2 < F - 1:
                            down_part(s - 1, n - FS - 2)
                        if ffn:
                            ffn_part(s, lo, o, n, at)
                        if prep:
                            prep_part(s, lo, o, n, at)
                        if exists(lo + 2):
                            early_part(s, lo, n, at)
                if with_scan:
                    for a in range(2):
                        transpose_state(s, NS - 1, a)
                if ffn:
                    down_part(s - 1, F - 1)
                if with_scan:
                    for a in range(2, NT):
                        transpose_state(s, NS - 1, a)
                if exists(lo + 2):
                    x_in(s, lo, 1)

            def early_part(s, lo, n, at):
                if (n, at) == (14, 1):
                    pe.wait_ge(norm["xa"].sem, norm["xa"].at(s + 2))
                    for k in range(KM):
                        pe.wait_ge(*ring_user_before(s, lo, "xt", k))
                        for a in range(NT):
                            last = nc.tensor.transpose(ring_bank("xt", k)[:, a * P:(a + 1) * P],
                                                       XA[:, a, k * P:(k + 1) * P], IDN[:, :])
                        last.then_inc(full["xt"].sem, 1)
                if (n, at) == (15, 1):
                    pe.wait_ge(xt.sem, xt.at(s + 2))
                    x_in(s, lo, 0)

            def x_in(s, lo, j):
                pe.wait_ge(*ring_user_before(s, lo, "xin", j))
                for k in range(KM):
                    last = nc.tensor.matmul(ring_bank("xin", j)[:, :], WIN[:, k, j * P:(j + 1) * P],
                                            XT[:, k, :], start=(k == 0), stop=(k == KM - 1))
                last.then_inc(full["xin"].sem, 1)

            def transpose_du(s, a):
                pe.wait_ge(*ht_user_before(s, a))
                for j in range(J):
                    last = nc.tensor.matmul(HT[a % HTS][:, j * P:(j + 1) * P],
                                            U[:, j, a * P:(a + 1) * P], DIAG[:, j, :],
                                            start=True, stop=True)
                last.then_inc(ht_full.sem, 1)

            def transpose_state(s, n, a):
                if a == 0:
                    pe.wait_ge(scan.sem, scan.at(s, (n + 1) * J))
                q = NT * (n + 1) + a
                pe.wait_ge(*ht_user_before(s, q))
                for j in range(J):
                    last = nc.tensor.transpose(HT[q % HTS][:, j * P:(j + 1) * P],
                                               H[:, n % 2, j, a * P:(a + 1) * P], IDN[:, :])
                last.then_inc(ht_full.sem, 1)

            def transpose_y(s, lo):
                pe.wait_ge(y_gate.sem, y_gate.at(s - 1))
                for j in range(J):
                    pe.wait_ge(*ring_user_before(s, lo, "yd", j))
                    bank = ring_bank("yd", j)
                    for a in range(NT):
                        last = nc.tensor.transpose(bank[:, a * P:(a + 1) * P],
                                                   YT[:, a, j * P:(j + 1) * P], IDN[:, :])
                    last.then_inc(full["yd"].sem, 1)

            def project_out(c, a):
                for j in range(J):
                    last = nc.tensor.matmul(DN[a // 2][:, (a % 2) * DM:(a % 2 + 1) * DM],
                                            SCR[:, j, a * P:(a + 1) * P], WO[:, j, :],
                                            start=(j == 0), stop=(j == J - 1))
                last.then_inc(o_full.sem, 1)

            def ffn_part(s, lo, o, n, at):
                c = s - 1
                if (n, at) == (0, 3):
                    pe.wait_ge(yd.sem, yd.at(c))
                    pe.wait_ge(resid["y"].sem, resid["y"].at(c - 1))
                    project_out(c, 0)
                if (n, at) == (1, 1):
                    project_out(c, 1)
                if (n, at) == (1, 2):
                    project_out(c, 2)
                    project_out(c, 3)
                if (n, at) == (4, 3):
                    pe.wait_ge(norm["x1"].sem, norm["x1"].at(c))
                    for k in range(KM):
                        pe.wait_ge(*ring_user_before(s, lo, "x1t", k))
                        bank = ring_bank("x1t", k)
                        for a in range(NT):
                            last = nc.tensor.transpose(bank[:, a * P:(a + 1) * P],
                                                       XN[:, a, k * P:(k + 1) * P], IDN[:, :])
                        last.then_inc(full["x1t"].sem, 1)
                if (n, at) == (FS, 1):
                    pe.wait_ge(x1t.sem, x1t.at(c))
                    pe.wait_ge(resid["o"].sem, resid["o"].at(c))
                    for a in range(NT):
                        for k in range(KM):
                            last = nc.tensor.matmul(DN[0][:, a * E:(a + 1) * E],
                                                    X1T[:, k, a * P:(a + 1) * P], WR[:, k, :],
                                                    start=(k == 0), stop=(k == KM - 1))
                    last.then_inc(rt_full.sem, 1)
                f = n - FS
                if 0 <= f < F and at == 1:
                    pe.wait_ge(hid.sem, hid.at(c, f))
                    for k in range(KM):
                        last = nc.tensor.matmul(GK[:, :], WG[:, k, f, :], X1T[:, k, :],
                                                start=(k == 0), stop=(k == KM - 1))
                    last.then_inc(gate_full.sem, 1)
                if 0 <= f < F and at == 2:
                    pe.wait_ge(*ring_user_before(s, lo, "up", f))
                    bank = ring_bank("up", f)
                    for k in range(KM):
                        last = nc.tensor.matmul(bank[:, :], WU[:, k, f, :], X1T[:, k, :],
                                                start=(k == 0), stop=(k == KM - 1))
                    last.then_inc(full["up"].sem, 1)
                if (n, at) == (FS + SH, 3):
                    pe.wait_ge(rt.sem, rt.at(c))
                    pe.wait_ge(*ring_user_before(s, lo, "cf", 0))
                    bank = ring_bank("cf", 0)
                    for a in range(NT):
                        last = nc.tensor.matmul(bank[0:E, a * P:(a + 1) * P], COEF[:, a, :],
                                                IDN[:, :], start=True, stop=True)
                    last.then_inc(full["cf"].sem, 1)

            def down_part(c, f):
                pe.wait_ge(hf.sem, hf.at(c, hf_done(f)))
                if f == 0:
                    pe.wait_ge(rt.sem, rt.at(c, 2))
                for a in range(NT):
                    last = nc.tensor.matmul(DN[a // 2][:, (a % 2) * DM:(a % 2 + 1) * DM],
                                            HF[:, a * P:(a + 1) * P], WD[:, f, :],
                                            start=(f == 0 and a % 2 == 0), stop=(f == F - 1),
                                            skip_group_check=True)
                last.then_inc(down.sem, 1)

            def prep_part(s, lo, o, n, at):
                c = s + 1

                def z(a):
                    pe.wait_ge(*ring_user_before(s, lo, "z", a))
                    for k in range(KM):
                        last = nc.tensor.matmul(ring_bank("z", a)[:, :], XT[:, k, a * P:(a + 1) * P],
                                                WIN[:, k, DI:2 * DI], start=(k == 0), stop=(k == KM - 1))
                    last.then_inc(full["z"].sem, 1)

                def delta(j):
                    pe.wait_ge(*ring_user_before(s, lo, "dl", j))
                    nc.tensor.matmul(ring_bank("dl", j)[:, :], WDT[ROW_DT:ROW_DT + RANK, j * P:(j + 1) * P],
                                     XD[ROW_DT:ROW_DT + RANK, o, :], start=True, stop=True)\
                      .then_inc(full["dl"].sem, 1)

                if (n, at) in Z_PE:
                    z(Z_PE.index((n, at)))
                if (n, at) in ((2, 3), (4, 1)):
                    x_in(s, lo, n // 2 + 1)
                if (n, at) in ((7, 3), (8, 1)):
                    if n == 7:
                        pe.wait_ge(*ring_user_before(s, lo, "xd", 0))
                    for j in (0, 1) if n == 7 else (2, 3):
                        pe.wait_ge(u_s.sem, u_s.at(c, j + 1))
                        last = nc.tensor.matmul(ring_bank("xd", 0)[0:XD_ROWS, :], WX[:, j, :], U[:, j, :],
                                                start=(j == 0), stop=(j == J - 1))
                    if n == 8:
                        last.then_inc(full["xd"].sem, 1)
                if (n, at) == (8, 3):
                    pe.wait_ge(xd.sem, xd.at(c))
                    delta(0)
                    delta(1)
                if (n, at) == (9, 1):
                    delta(2)
                    delta(3)
                if (n, at) == (13, 3):
                    pe.wait_ge(*ring_user_before(s, lo, "ct", 0))
                    for a in range(NT):
                        last = nc.tensor.matmul(ring_bank("ct", 0)[:, a * NS:(a + 1) * NS],
                                                XD[ROW_C:ROW_C + NS, o, a * P:(a + 1) * P],
                                                IDN[ROW_C:ROW_C + NS, ROW_C:ROW_C + NS],
                                                start=True, stop=True)
                    last.then_inc(full["ct"].sem, 1)

            run(pe, body)

        @block.scalar
        def _(act):
            act.wait_ge(const_ld.sem, CONST_LOADS)
            nc.scalar.activation(ANEG[:, :, :], ANEG[:, :, :], ACT.Exp).then_inc(a_exp.sem, 1)
            act.wait_ge(consts.sem, 1)

            def decay(s, r, n, j):
                if n == 0:
                    act.wait_ge(scan.sem, scan.at(s - 1, (NS - 1) * J + j + 1))
                    act.wait_ge(lsum.sem, lsum.at(s, j + 1))
                else:
                    act.wait_ge(scan.sem, scan.at(s, (n - 1) * J + j + 1))
                nc.scalar.activation(DA[:, j, :], DL[:, r, j, :], ACT.Exp,
                                     scale=ANEG[:, j, n:n + 1]).then_inc(ex.sem, 1)

            def rsqrt(w, c):
                used = (norm if w in norm else resid)[w]
                act.wait_ge(stats[w].sem, stats[w].at(c))
                act.wait_ge(used.sem, used.at(c - 1))
                nc.scalar.activation(RS[w][:, :], MV[w][:, :, 1], ACT.Ln, bias=EPST[:, 0:1])\
                  .then_inc(rstd[w].sem, 1)
                act.wait_ge(rstd[w].sem, rstd[w].at(c, 1))
                nc.scalar.activation(RS[w][:, :], RS[w][:, :], ACT.Exp, scale=-0.5)\
                  .then_inc(rstd[w].sem, 1)

            def mean_rstd(w, c):
                act.wait_ge(rstd[w].sem, rstd[w].at(c))
                for a in range(NT):
                    nc.scalar.activation(MR[w][:, a:a + 1], MV[w][:, a, 0:1], ACT.Identity,
                                         scale=RS[w][:, a:a + 1]).then_inc(shift[w].sem, 1)

            def minus_mean_rstd(w, c):
                mean_rstd(w, c)
                act.wait_ge(shift[w].sem, shift[w].at(c, NT))
                nc.scalar.activation(MR[w][:, :], MR[w][:, :], ACT.Identity, scale=-1.0)\
                  .then_inc(shift[w].sem, 1)
                act.wait_ge(shift[w].sem, shift[w].at(c))

            def normed(w, c, dst, src):
                minus_mean_rstd(w, c)
                for a in range(NT):
                    nc.scalar.activation(dst[:, a, :], src[:, a, :], ACT.Identity,
                                         bias=MR[w][:, a:a + 1], scale=RS[w][:, a:a + 1])\
                      .then_inc(norm[w].sem, 1)

            def shifted_stream(c):
                mean_rstd("o", c)
                act.wait_ge(xr_ld.sem, xr_ld.at(c))
                for a in range(NT):
                    act.wait_ge(shift["o"].sem, shift["o"].at(c, a + 1))
                    nc.scalar.activation(XR[:, a, :], XR[:, a, :], ACT.Identity,
                                         bias=MR["o"][:, a:a + 1], scale=-1.0).then_inc(stream["o"].sem, 1)

            def shift_result(c):
                minus_mean_rstd("y", c)
                for a in range(NT):
                    act.wait_ge(resid["y"].sem, resid["y"].at(c, a + 1))
                    nc.scalar.activation(XR[:, a, :], XR[:, a, :], ACT.Identity,
                                         bias=MR["y"][:, a:a + 1]).then_inc(stream["y"].sem, 1)

            def body(s, lo, r):
                with_scan, ffn, prep = parts(lo)
                o = 1 - r
                if ffn:
                    y_take(s, lo)
                if with_scan:
                    for a in range(NT):
                        act.wait_ge(ht_full.sem, ht_full.at(s, a + 1))
                        act.wait_ge(full["yd"].sem, full["yd"].at(s - 1))
                        nc.scalar.activation(YT[:, a, :], HT[a % HTS][:, :], ACT.Copy)\
                          .then_inc(yinit.sem, 1)
                        if a == 0:
                            decay(s, r, 1, 0)
                for n in range(NS):
                    for at in range(J):
                        if with_scan and n + 1 < NS and (n, at) != (0, 0):
                            decay(s, r, n + 1, at)
                        if prep and n + 1 == NS:
                            decay(s + 1, o, 0, at)
                        if exists(lo - 2) and (n, at) == (1, 0):
                            shift_result(s - 2)
                        if ffn:
                            ffn_part(s, lo, o, n, at)
                        if prep:
                            prep_part(s, lo, o, n, at)
                        if exists(lo + 2):
                            early_part(s, r, n, at)
                if ffn:
                    rsqrt("y", s - 1)
                if exists(lo + 2):
                    x_in(s + 2, 1)

            def early_part(s, r, n, at):
                c = s + 2
                if (n, at) == (10, 3):
                    rsqrt("xa", c)
                if (n, at) == (11, 3):
                    normed("xa", c, XA, XA)
                if (n, at) == (14, 1):
                    for k in range(KM):
                        act.wait_ge(full["xt"].sem, full["xt"].at(c, k + 1))
                        act.wait_ge(dadd.sem, dadd.at(c - 1))
                        act.wait_ge(dadd_v.sem, dadd_v.at(c - 1))
                        nc.scalar.activation(XT[:, k, :], ring_bank("xt", k)[:, :], ACT.Copy)\
                          .then_inc(xt.sem, 1)
                if (n, at) == (15, 0):
                    act.wait_ge(conv.sem, conv.at(c - 1))
                    act.wait_ge(halo.sem, halo.at(c - 1))
                    nc.scalar.activation(XIN[:, :, 0:TAPS - 1], HALO[:, r, :, :], ACT.Copy)\
                      .then_inc(halo.sem, 1)
                if (n, at) == (15, 2):
                    x_in(c, 0)

            def x_in(c, j):
                act.wait_ge(full["xin"].sem, full["xin"].at(c, j + 1))
                act.wait_ge(conv.sem, conv.at(c - 1))
                nc.scalar.activation(XIN[:, j, TAPS - 1:], ring_bank("xin", j)[:, :], ACT.Copy)\
                  .then_inc(xin.sem, 1)

            def y_take(s, lo):
                for j in range(J):
                    act.wait_ge(full["yd"].sem, full["yd"].at(s - 1, j + 1))
                    if parts(lo)[0]:
                        act.wait_ge(lsum.sem, lsum.at(s))
                    nc.scalar.activation(SCR[:, j, :], ring_bank("yd", j)[:, :], ACT.Copy)\
                      .then_inc(yd.sem, 1)

            def ffn_part(s, lo, o, n, at):
                c = s - 1
                if (n, at) == (2, 1):
                    rsqrt("o", c)
                if (n, at) == (2, 2):
                    shifted_stream(c)
                if (n, at) == (3, 3):
                    rsqrt("x1", c)
                if (n, at) == (4, 3):
                    for k in range(KM):
                        act.wait_ge(full["x1t"].sem, full["x1t"].at(c, k + 1))
                        act.wait_ge(full["up"].sem, full["up"].at(c - 1))
                        nc.scalar.activation(X1T[:, k, :], ring_bank("x1t", k)[:, :], ACT.Copy)\
                          .then_inc(x1t.sem, 1)
                if (n, at) == (FS + 1, 0):
                    act.wait_ge(rt.sem, rt.at(c, 2))
                    nc.scalar.activation(RP[:, :, :], RP[:, :, :], ACT.Exp).then_inc(rex.sem, 1)
                f = n - FS
                if 0 <= f < F and at == 2:
                    act.wait_ge(gate_full.sem, gate_full.at(c, f + 1))
                    act.wait_ge(hf.sem, hf.at(c, up_used(f - 1)))
                    nc.scalar.activation(TG[:, :], GK[:, :], ACT.Tanh).then_inc(tg.sem, 1)
                if 0 <= f < F and at == 2:
                    act.wait_ge(full["up"].sem, full["up"].at(c, f + 1))
                    nc.scalar.activation(UP[:, :], ring_bank("up", f)[:, :], ACT.Copy)\
                      .then_inc(up.sem, 1)
                if (n, at) == (FS + SH, 3):
                    act.wait_ge(full["cf"].sem, full["cf"].at(c))
                    nc.scalar.activation(XD[ROW_K:ROW_K + E, o, :], ring_bank("cf", 0)[0:E, :],
                                         ACT.Copy).then_inc(cff.sem, 1)

            def prep_part(s, lo, o, n, at):
                c = s + 1

                def z(a):
                    act.wait_ge(full["z"].sem, full["z"].at(c, a + 1))
                    act.wait_ge(sz.sem, sz.at(c, a))
                    nc.scalar.activation(TZ[:, :], ring_bank("z", a)[:, :], ACT.Tanh)\
                      .then_inc(tz.sem, 1)
                    nc.scalar.activation(ZC[:, :], ring_bank("z", a)[:, :], ACT.Copy)\
                      .then_inc(tz.sem, 1)
                    act.wait_ge(tz.sem, tz.at(c, 3 * a + 1))
                    nc.scalar.activation(TZ[:, :], TZ[:, :], ACT.Identity, bias=ONE[:, 0:1])\
                      .then_inc(tz.sem, 1)

                def delta(j):
                    act.wait_ge(full["dl"].sem, full["dl"].at(c, j + 1))
                    if j == 0:
                        act.wait_ge(du.sem, du.at(c - 2))
                        act.wait_ge(full["z"].sem, full["z"].at(c))
                        if parts(lo)[1]:
                            act.wait_ge(full["x1t"].sem, full["x1t"].at(s - 1))
                    nc.scalar.activation(ZB[:, j, :], ring_bank("dl", j)[:, :], ACT.Abs,
                                         bias=BDT[:, j:j + 1]).then_inc(absrelu.sem, 1)
                    nc.scalar.activation(DL[:, o, j, :], ring_bank("dl", j)[:, :], ACT.Relu,
                                         bias=BDT[:, j:j + 1]).then_inc(absrelu.sem, 1)

                if (n, at) in Z_ACT:
                    z(Z_ACT.index((n, at)))
                if (n, at) in ((3, 0), (4, 2)):
                    x_in(c, n - 1)
                if (n, at) == (4, 2):
                    act.wait_ge(xin.sem, xin.at(c))
                    nc.scalar.activation(HALO[:, o, :, :], XIN[:, :, T:], ACT.Copy).then_inc(halo.sem, 1)
                if 1 <= n < 1 + J and at == 3:
                    j = n - 1
                    act.wait_ge(xin.sem, xin.at(c, j + 1))
                    act.wait_ge(halo.sem, halo.at(c, 1))
                    act.wait_ge(lsum.sem, lsum.at(c - 1))
                    if parts(lo)[1]:
                        act.wait_ge(o_full.sem, o_full.at(s - 1))
                    nc.scalar.activation(SCR[:, j, :], XIN[:, j, 0:T], ACT.Identity,
                                         bias=CB_[:, j:j + 1], scale=CW[:, j, 0:1])\
                      .then_inc(tap0.sem, 1)
                if (n, at) in TANH_CONV:
                    j = TANH_CONV.index((n, at))
                    act.wait_ge(conv.sem, conv.at(c, (TAPS - 1) * (j + 1)))
                    act.wait_ge(u_s.sem, u_s.at(c, j))
                    nc.scalar.activation(TC[:, :], SCR[:, j, :], ACT.Tanh).then_inc(tc.sem, 1)
                    act.wait_ge(tc.sem, tc.at(c, 2 * j + 1))
                    nc.scalar.activation(TC[:, :], TC[:, :], ACT.Identity, bias=ONE[:, 0:1])\
                      .then_inc(tc.sem, 1)
                if (n, at) == (8, 1):
                    act.wait_ge(full["xd"].sem, full["xd"].at(c))
                    for i in range(2):
                        act.wait_ge(bb_ld[i].sem, bb_ld[i].at(c - 2))
                    nc.scalar.activation(XD[0:XD_ROWS, o, :], ring_bank("xd", 0)[0:XD_ROWS, :], ACT.Copy)\
                      .then_inc(xd.sem, 1)
                if (n, at) == (8, 3):
                    delta(0)
                    delta(1)
                if (n, at) == (9, 1):
                    delta(2)
                    delta(3)
                if (n, at) == (14, 0):
                    act.wait_ge(full["ct"].sem, full["ct"].at(c))
                    act.wait_ge(add_c.sem, add_c.at(c - 2))
                    nc.scalar.activation(CT[:, o, :, :].rearrange("p a n -> p (a n)"),
                                         ring_bank("ct", 0)[:, 0:NT * NS], ACT.Copy).then_inc(ct.sem, 1)
                if n == 9 and at in (0, 2):
                    h = at // 2
                    blocks = slice(2 * h, 2 * h + 2)
                    act.wait_ge(absrelu.sem, absrelu.at(c, 4 * (h + 1)))
                    nc.scalar.activation(ZB[:, blocks, :], ZB[:, blocks, :], ACT.Exp, scale=-1.0)\
                      .then_inc(zex.sem, 1)
                    act.wait_ge(zex.sem, zex.at(c, h + 1))
                    act.wait_ge(u_s.sem, u_s.at(c))
                    nc.scalar.activation(SCR[:, blocks, :], ZB[:, blocks, :], ACT.Identity,
                                         bias=ONE[:, 0:1]).then_inc(wexp.sem, 1)
                if (n, at) == (10, 3):
                    act.wait_ge(corr.sem, corr.at(c))
                    nc.scalar.activation(SCR[:, :, :], SCR[:, :, :], ACT.Ln).then_inc(ln.sem, 1)

            run(act, body)

        @block.vector
        def _(dve):
            nc.vector.memset(WX[:, :, :], 0.0)
            nc.vector.memset(HALO[:, :, :, :], 0.0)
            nc.vector.memset(CARRY[:, :, :, :], 0.0)
            nc.vector.memset(ONE[:, :], 1.0)
            nc.vector.memset(EPST[:, :], EPS).then_inc(zeroed.sem, 1)
            dve.wait_ge(const_ld.sem, CONST_LOADS)
            dve.wait_ge(ident_made.sem, IDENT_MADE)
            dve.wait_ge(a_exp.sem, 1)
            nc.vector.tensor_scalar(WIN[:, :, DI:2 * DI], WIN[:, :, DI:2 * DI], 0.5, None, ALU.mult)
            nc.vector.tensor_scalar(CW[:, :, :], CW[:, :, :], 0.5, None, ALU.mult)
            nc.vector.tensor_scalar(CB_[:, :], CB_[:, :], 0.5, None, ALU.mult)
            nc.vector.tensor_scalar(ANEG[:, :, :], ANEG[:, :, :], -1.0, None, ALU.mult)
            for j in range(J):
                last = nc.vector.tensor_scalar(DIAG[:, j, :], IDN[:, :], DSK[:, j:j + 1], None, ALU.mult)
            last.then_inc(consts.sem, 1)
            dve.wait_ge(consts.sem, 1)

            def scan_step(s, r, n, j):
                dve.wait_ge(ex.sem, ex.at(s, n * J + j + 1))
                if j % 2 == 0:
                    dve.wait_ge(bu.sem, bu.at(s, 2 * n + j // 2 + 1))
                if j == 0:
                    if n < 2:
                        dve.wait_ge(ht_full.sem, ht_full.at(s - 1, NT * (NS + n)))
                    else:
                        dve.wait_ge(ht_full.sem, ht_full.at(s, NT * n))
                    dve.wait_ge(carry.sem, carry.at(s, n))
                nc.vector.tensor_tensor_scan(H[:, n % 2, j, :], DA[:, j, :],
                                             BU[:, (2 * n + j // 2) % 4, j % 2, :],
                                             CARRY[:, r, n, j:j + 1], ALU.mult, ALU.add)\
                  .then_inc(scan.sem, 1)

            def add_state(s, r, n, a):
                dve.wait_ge(ht_full.sem, ht_full.at(s, NT * (n + 1) + a + 1))
                if n == 0:
                    dve.wait_ge(yinit.sem, yinit.at(s, a + 1))
                    dve.wait_ge(ct.sem, ct.at(s))
                else:
                    dve.wait_ge(add_c.sem, add_c.at(s, (n - 1) * NT + a + 1))
                nc.vector.scalar_tensor_tensor(YT[:, a, :], HT[(NT * (n + 1) + a) % HTS][:, :],
                                               CT[:, r, a, n:n + 1], YT[:, a, :],
                                               ALU.mult, ALU.add).then_inc(add_c.sem, 1)

            def moments(w, c, a, tile):
                nc.vector.bn_stats(ST[w][:, a, :], tile).then_inc(stats[w].sem, 1)

            def moments_end(w, c):
                dve.wait_ge(stats[w].sem, stats[w].at(c, NT))
                used = (shift if w in shift else rstd)[w]
                dve.wait_ge(used.sem, used.at(c - 1))
                dve.sem_inc(waited, 1)
                for a in range(NT):
                    nc.vector.bn_aggr(MV[w][:, a, :], ST[w][:, a, :]).then_inc(stats[w].sem, 1)

            def add_stream_o(c, a):
                dve.wait_ge(stream["o"].sem, stream["o"].at(c, a + 1))
                nc.vector.scalar_tensor_tensor(XR[:, a, :], dn(a), RS["o"][:, a:a + 1], XR[:, a, :],
                                               ALU.mult, ALU.subtract).then_inc(resid["o"].sem, 1)

            def add_stream_y(c, a):
                dve.wait_ge(rstd["y"].sem, rstd["y"].at(c))
                nc.vector.scalar_tensor_tensor(XR[:, a, :], dn(a), RS["y"][:, a:a + 1], XR[:, a, :],
                                               ALU.mult, ALU.add).then_inc(resid["y"].sem, 1)

            def dn(a):
                return DN[a // 2][:, (a % 2) * DM:(a % 2 + 1) * DM]

            def body(s, lo, r):
                with_scan, ffn, prep = parts(lo)
                if lo == 0:
                    dve.wait_ge(ffn_ld.sem, FFN_LOADS)
                    nc.vector.tensor_scalar(WG[:, :, :, :], WG[:, :, :, :], 0.5, None, ALU.mult)\
                      .then_inc(ffn_consts.sem, 1)
                o = 1 - r
                for n in range(NS):
                    for j in range(J):
                        if with_scan:
                            scan_step(s, r, n, j)
                        side_part(s, lo, o, n, 2 * j)
                        if with_scan and n > 0:
                            add_state(s, r, n - 1, j)
                        side_part(s, lo, o, n, 2 * j + 1)
                    if with_scan:
                        dve.wait_ge(scan.sem, scan.at(s, (n + 1) * J))
                        nc.vector.tensor_copy(CARRY[:, r, n, :], H[:, n % 2, :, T - 1])\
                          .then_inc(carry.sem, 1)
                    if ffn:
                        ffn_end(s, lo, n)
                if with_scan:
                    for a in range(2):
                        add_state(s, r, NS - 1, a)
                if ffn:
                    for a in range(NT):
                        dve.wait_ge(down.sem, down.at(s - 1))
                        moments("y", s - 1, a, dn(a))
                    moments_end("y", s - 1)
                if with_scan:
                    for a in range(2, NT):
                        add_state(s, r, NS - 1, a)
                if with_scan:
                    for a in range(NT):
                        dve.wait_ge(add_c.sem, add_c.at(s, (NS - 1) * NT + a + 1))
                        dve.wait_ge(sz.sem, sz.at(s))
                        nc.vector.tensor_tensor(YT[:, a, :], YT[:, a, :], SZ[:, r, a, :], ALU.mult)\
                          .then_inc(y_gate.sem, 1)

            def over(t):
                return t.unsqueeze(2).to_broadcast([P, NT, E])

            def side_part(s, lo, o, n, pos):
                if exists(lo - 2) and n == 0 and pos >= 8 - NT:
                    add_stream_y(s - 2, pos - (8 - NT))
                if exists(lo - 1):
                    ffn_part(s, lo, o, n, pos)
                if exists(lo + 1):
                    prep_part(s, lo, o, n, pos)
                if exists(lo + 2) and n == 9 and pos % 2 == 0:
                    a = pos // 2
                    dve.wait_ge(xa_ld.sem, xa_ld.at(s + 2))
                    moments("xa", s + 2, a, XA[:, a, :])
                if exists(lo + 2) and (n, pos) == (9, 7):
                    moments_end("xa", s + 2)

            def route(c, i):
                if i == 2:
                    dve.wait_ge(rex.sem, rex.at(c))
                elif i > 0:
                    dve.wait_ge(rt.sem, rt.at(c, i))
                logits = DN[0][:, 0:NT * E].rearrange("p (a e) -> p a e", a=NT)
                if i == 0:
                    dve.wait_ge(rt_full.sem, rt_full.at(c))
                    last = nc.vector.tensor_reduce(RMAX, logits, X, ALU.max)
                elif i == 1:
                    last = nc.vector.tensor_tensor(RP[:, :, :], logits, over(RMAX), ALU.subtract)
                elif i == 2:
                    last = nc.vector.tensor_reduce(RSUM, RP[:, :, :], X, ALU.add)
                elif i == 3:
                    last = nc.vector.reciprocal(RINV, RSUM)
                elif i == 4:
                    last = nc.vector.tensor_tensor(RP[:, :, :], RP[:, :, :], over(RINV), ALU.mult)
                elif i in (5, 11):
                    src = RP if i == 5 else RL
                    last = nc.vector.tensor_reduce(R1, src[:, :, :], X, ALU.max)
                elif i in (6, 12):
                    src = RP if i == 6 else RL
                    last = nc.vector.tensor_tensor(RQ[:, :, :], src[:, :, :], over(R1), ALU.is_equal)
                elif i in (7, 13):
                    last = nc.vector.tensor_tensor(RQ[:, :, :], RQ[:, :, :], RANKS[:, :].unsqueeze(1).to_broadcast([P, NT, E]), ALU.mult)
                elif i in (8, 14):
                    last = nc.vector.tensor_reduce(R1, RQ[:, :, :], X, ALU.max)
                elif i in (9, 15):
                    dst = RM if i == 9 else RQ
                    last = nc.vector.tensor_tensor(dst[:, :, :], RQ[:, :, :], over(R1), ALU.is_equal)
                elif i == 10:
                    last = nc.vector.scalar_tensor_tensor(RL[:, :, :], RM[:, :, :], -4.0, RP[:, :, :],
                                                          ALU.mult, ALU.add)
                elif i == 16:
                    last = nc.vector.tensor_tensor(RM[:, :, :], RM[:, :, :], RQ[:, :, :], ALU.add)
                else:
                    last = nc.vector.tensor_tensor(COEF[:, :, :], RM[:, :, :], RP[:, :, :], ALU.mult)
                last.then_inc(rt.sem, 1)

            def ffn_part(s, lo, o, n, pos):
                c = s - 1
                a = {(1, 6): 0, (1, 7): 2}.get((n, pos))
                if a is not None:
                    dve.wait_ge(o_full.sem, o_full.at(c, a + 2))
                    moments("o", c, a, dn(a))
                    moments("o", c, a + 1, dn(a + 1))
                if (n, pos) == (2, 0):
                    moments_end("o", c)
                if n == 3 and pos < NT:
                    add_stream_o(c, pos)
                if n == 3 and 2 <= pos < 2 + NT:
                    a = pos - 2
                    dve.wait_ge(resid["o"].sem, resid["o"].at(c, a + 1))
                    moments("x1", c, a, XR[:, a, :])
                if (n, pos) == (3, 6):
                    moments_end("x1", c)
                if n == 4 and 1 <= pos < 1 + NT:
                    a = pos - 1
                    if a == 0 and parts(lo)[0]:
                        dve.wait_ge(dadd.sem, dadd.at(s))
                        dve.wait_ge(dadd_v.sem, dadd_v.at(s))
                    dve.wait_ge(rstd["x1"].sem, rstd["x1"].at(c))
                    nc.vector.tensor_scalar(XN[:, a, :], XR[:, a, :], MV["x1"][:, a, 0:1],
                                            RS["x1"][:, a:a + 1], ALU.subtract, ALU.mult)\
                      .then_inc(norm["x1"].sem, 1)
                place = 8 * (n - FS - 1) + pos - 3
                if place >= 0:
                    for i in range(2 + 2 * place, min(4 + 2 * place, RT_STEPS)):
                        route(c, i)
                f = n - FS - 1
                if 0 <= f < F and pos == 0:
                    dve.wait_ge(tg.sem, tg.at(c, f + 1))
                    nc.vector.scalar_tensor_tensor(TG[:, :], TG[:, :], 1.0, GK[:, :],
                                                   ALU.add, ALU.mult).then_inc(hid.sem, 1)

            def ffn_end(s, lo, n):
                c = s - 1
                if n == FS:
                    route(c, 0)
                    route(c, 1)
            def prep_part(s, lo, o, n, pos):
                c = s + 1
                for j in range(J):
                    if (n, pos) in TAP[j]:
                        k = 1 + TAP[j].index((n, pos))
                        if k == 1:
                            dve.wait_ge(tap0.sem, tap0.at(c, j + 1))
                        else:
                            dve.wait_ge(conv.sem, conv.at(c, (TAPS - 1) * j + k - 1))
                        nc.vector.scalar_tensor_tensor(SCR[:, j, :], XIN[:, j, k:k + T],
                                                       CW[:, j, k:k + 1], SCR[:, j, :],
                                                       ALU.mult, ALU.add).then_inc(conv.sem, 1)
                if n == 10 and pos % 2 == 0:
                    j = pos // 2
                    dve.wait_ge(wexp.sem, wexp.at(c, j // 2 + 1))
                    nc.vector.scalar_tensor_tensor(ZB[:, j, :], SCR[:, j, :], -1.0, ZB[:, j, :],
                                                   ALU.add, ALU.subtract).then_inc(corr.sem, 1)
                if (n, pos) == (13, 2):
                    dve.wait_ge(corr.sem, corr.at(c))
                    nc.vector.tensor_tensor(DL[:, o, J - 1, :], DL[:, o, J - 1, :], ZB[:, J - 1, :],
                                            ALU.subtract).then_inc(dadd_v.sem, 1)
                if (n, pos) in LSUM_AT:
                    j = LSUM_AT.index((n, pos))
                    dve.wait_ge(ln.sem, ln.at(c))
                    if j < J - 1:
                        dve.wait_ge(dadd.sem, dadd.at(c, j + 1))
                    else:
                        dve.wait_ge(dadd_v.sem, dadd_v.at(c))
                    nc.vector.tensor_tensor(DL[:, o, j, :], DL[:, o, j, :], SCR[:, j, :], ALU.add)\
                      .then_inc(lsum.sem, 1)

            run(dve, body)

        @block.gpsimd
        def _(pool):
            nc.gpsimd.memset(IDN[:, :], 0.0).then_inc(ident_made.sem, 1)
            pool.wait_ge(ident_made.sem, 1)
            nc.gpsimd.affine_select(out=IDN[:, :], in_=IDN[:, :], compare_op=ALU.not_equal, fill=1.0,
                                    base=0, pattern=[[-1, P]], channel_multiplier=1)\
              .then_inc(ident_made.sem, 1)
            for e in range(E):
                nc.gpsimd.memset(RANKS[:, e:e + 1], float(E - e)).then_inc(ident_made.sem, 1)

            def inflow(s, n, h):
                pool.wait_ge(bb_ld[n % 2].sem, bb_ld[n % 2].at(s, 16 * (n // 2 + 1)))
                if n == 0:
                    pool.wait_ge(du.sem, du.at(s, 2 * h + 2))
                if n < 2:
                    pool.wait_ge(scan.sem, scan.at(s - 1, (n + NS - 2) * J + 2 * h + 2))
                else:
                    pool.wait_ge(scan.sem, scan.at(s, (n - 2) * J + 2 * h + 2))
                nc.gpsimd.tensor_tensor(BU[:, (2 * n + h) % 4, :, :], DU[:, 2 * h:2 * h + 2, :],
                                        BB[:, n % 2, :].unsqueeze(1).to_broadcast([P, 2, T]),
                                        ALU.mult).then_inc(bu.sem, 1)

            def body(s, lo, r):
                with_scan, ffn, prep = parts(lo)
                o = 1 - r
                for n in range(NS):
                    if with_scan and n + 1 < NS:
                        inflow(s, n + 1, 0)
                    f = n - FS - 1
                    if ffn and 0 <= f < F:
                        hidden(s - 1, f)
                    if with_scan and n + 1 < NS:
                        inflow(s, n + 1, 1)
                    if prep:
                        prep_part(s + 1, s, o, n)

            def hidden(c, f):
                pool.wait_ge(hid.sem, hid.at(c, f + 1))
                pool.wait_ge(up.sem, up.at(c, f + 1))
                pool.wait_ge(down.sem, down.at(c, f))
                nc.gpsimd.tensor_tensor(HF[:, :], TG[:, :], UP[:, :], ALU.mult).then_inc(hf.sem, 1)
                if f >= SH:
                    pool.wait_ge(hf.sem, hf.at(c, hf_done(f) - 1))
                    e = f - SH
                    pool.wait_ge(cb_ld[e % 2].sem, cb_ld[e % 2].at(c, 16 * (e // 2 + 1)))
                    nc.gpsimd.tensor_tensor(HF[:, :], HF[:, :], CB[:, e % 2, :], ALU.mult)\
                      .then_inc(hf.sem, 1)

            def prep_part(c, s, o, n):
                if 4 <= n < 4 + J:
                    j = n - 4
                    pool.wait_ge(tc.sem, tc.at(c, 2 * (j + 1)))
                    if j == 0:
                        pool.wait_ge(ht_full.sem, ht_full.at(s, NT))
                        pool.wait_ge(du.sem, du.at(s))
                    nc.gpsimd.tensor_tensor(U[:, j, :], TC[:, :], SCR[:, j, :], ALU.mult)\
                      .then_inc(u_s.sem, 1)
                if n in SZ_POOL:
                    a = SZ_POOL.index(n)
                    pool.wait_ge(tz.sem, tz.at(c, 3 * (a + 1)))
                    if a == 0:
                        pool.wait_ge(y_gate.sem, y_gate.at(s - 1))
                    nc.gpsimd.tensor_tensor(SZ[:, o, a, :], TZ[:, :], ZC[:, :], ALU.mult)\
                      .then_inc(sz.sem, 1)
                if 10 <= n < 10 + J - 1:
                    j = n - 10
                    pool.wait_ge(corr.sem, corr.at(c, j + 1))
                    nc.gpsimd.tensor_tensor(DL[:, o, j, :], DL[:, o, j, :], ZB[:, j, :], ALU.subtract)\
                      .then_inc(dadd.sem, 1)
                if n == 15:
                    for j in range(J):
                        pool.wait_ge(lsum.sem, lsum.at(c, j + 1))
                        pool.wait_ge(u_s.sem, u_s.at(c))
                        if j == 0:
                            pool.wait_ge(bu.sem, bu.at(s))
                        nc.gpsimd.tensor_tensor(DU[:, j, :], DL[:, o, j, :], U[:, j, :], ALU.mult)\
                          .then_inc(du.sem, 1)
                        if j % 2 == 1:
                            inflow(c, 0, j // 2)

            run(pool, body)


_INS = ["L0_attn_x", "L0_attn_W_in", "L0_attn_conv_w", "L0_attn_conv_b", "L0_attn_W_xproj",
        "L0_attn_W_dt", "L0_attn_b_dt", "L0_attn_A_log", "L0_attn_D_skip", "L0_attn_W_out",
        "L0_ffn_router", "L0_ffn_experts_gate", "L0_ffn_experts_up", "L0_ffn_experts_down",
        "L0_ffn_shared_gate", "L0_ffn_shared_up", "L0_ffn_shared_down"]


def kernel(**inputs):
    import numpy as _np
    import concourse.bacc as _bacc
    from concourse import mybir as _mybir
    from concourse.bass_utils import run_bass_kernel_spmd as _run

    nc = _bacc.Bacc("TRN2", target_bir_lowering=False, num_devices=1)
    arrays, args = {}, []
    for name in _INS:
        a = _np.ascontiguousarray(inputs[name])
        arrays[name + "_in"] = a
        args.append(nc.dram_tensor(name + "_in", a.shape, _mybir.dt.from_np(a.dtype),
                                   kind="ExternalInput").ap())
    shape = inputs["L0_attn_x"].shape
    args.append(nc.dram_tensor("out", shape, _mybir.dt.float32, kind="ExternalOutput").ap())
    mamba_moe_kernel(nc, *args)
    r = _run(nc, [arrays], core_ids=[0])
    return r.results[0]["out"]
```
